# Optimizing a Trainium2 kernel written in Bass

```python
import numpy as np
import jax
import jax.numpy as jnp

def _softmax(x, axis=-1):
    return jax.nn.softmax(x, axis=axis)
def _gelu(x):
    return jax.nn.gelu(x, approximate=True)
def _silu(x):
    return jax.nn.silu(x)
def _sigmoid(x):
    return jax.nn.sigmoid(x)
def _layernorm(x, axis=-1, eps=1e-5):
    m = jnp.mean(x, axis=axis, keepdims=True)
    v = jnp.var(x, axis=axis, keepdims=True)
    return (x - m) / jnp.sqrt(v + eps)
def _scatter_add(tgt, idx, src, axis=0):
    return tgt.at[idx].add(src)
def _segment_sum(src, seg, n):
    return jax.ops.segment_sum(src, seg, n)

kernel_name = 'mk_conv_preact_d2_conv_nhwc256_e36c79'

def setup_inputs(seed: int = 0):
    np.random.seed(seed)
    _w = jnp.asarray
    def _rec_inputs():
        import jax
        import jax.numpy as jnp
        _gk = jax.random.key(seed)
        x = -0.0003929 + 0.9999 * jax.random.normal(jax.random.fold_in(_gk, 1), (64, 64, 16, 256), jnp.float32)
        return x
    x = _rec_inputs()
    def _L0_conv_setup():
        import jax, jax.numpy as jnp
        import numpy as np
        H, W, B, D = (64, 64, 16, 256)

        def _scan(inp, lam, axis):

            def combine(a, b):
                la, ia = a
                lb, ib = b
                return (la * lb, lb * ia + ib)
            return jax.lax.associative_scan(combine, (lam, inp), axis=axis)[1]

        def _bidir(inp, lam, axis):
            fwd = _scan(inp, lam, axis)
            rev = jnp.flip(_scan(jnp.flip(inp, axis), jnp.flip(lam, axis), axis), axis)
            return fwd + rev
        key = jax.random.key(seed)
        ks = jax.random.split(key, 9)
        s = 1.0 / np.sqrt(D)
        inp = {'x': jax.random.normal(ks[0], (H, W, B, D), jnp.float32)}
        for i, n in enumerate(['Wi', 'Wl', 'Wg', 'Wo']):
            inp[n] = jax.random.uniform(ks[1 + i], (D, D), jnp.float32, -s, s)
        for i, n in enumerate(['bi', 'bl', 'bg', 'bo']):
            inp[n] = jax.random.uniform(ks[5 + i], (D,), jnp.float32, -s, s)
        inp['gamma'] = jnp.ones((D,), jnp.float32)
        inp['beta'] = jnp.zeros((D,), jnp.float32)
        inp['lower_bound'] = 0
        return inp
    _L0_conv_all = _L0_conv_setup()
    _L0_conv_in = {k: v for k, v in _L0_conv_all.items() if k in ('Wi', 'bi', 'Wl', 'bl', 'Wg', 'bg', 'Wo', 'bo', 'gamma', 'beta', )}
    del _L0_conv_all

    def _L1_conv_setup():
        import jax, jax.numpy as jnp
        import numpy as np
        H, W, B, D = (64, 64, 16, 256)

        def _scan(inp, lam, axis):

            def combine(a, b):
                la, ia = a
                lb, ib = b
                return (la * lb, lb * ia + ib)
            return jax.lax.associative_scan(combine, (lam, inp), axis=axis)[1]

        def _bidir(inp, lam, axis):
            fwd = _scan(inp, lam, axis)
            rev = jnp.flip(_scan(jnp.flip(inp, axis), jnp.flip(lam, axis), axis), axis)
            return fwd + rev
        key = jax.random.key(seed)
        ks = jax.random.split(key, 9)
        s = 1.0 / np.sqrt(D)
        inp = {'x': jax.random.normal(ks[0], (H, W, B, D), jnp.float32)}
        for i, n in enumerate(['Wi', 'Wl', 'Wg', 'Wo']):
            inp[n] = jax.random.uniform(ks[1 + i], (D, D), jnp.float32, -s, s)
        for i, n in enumerate(['bi', 'bl', 'bg', 'bo']):
            inp[n] = jax.random.uniform(ks[5 + i], (D,), jnp.float32, -s, s)
        inp['gamma'] = jnp.ones((D,), jnp.float32)
        inp['beta'] = jnp.zeros((D,), jnp.float32)
        inp['lower_bound'] = 0
        return inp
    _L1_conv_all = _L1_conv_setup()
    _L1_conv_in = {k: v for k, v in _L1_conv_all.items() if k in ('Wi', 'bi', 'Wl', 'bl', 'Wg', 'bg', 'Wo', 'bo', 'gamma', 'beta', )}
    del _L1_conv_all

    return {
        "x": x,
        "L0_conv_Wi": _L0_conv_in["Wi"],
        "L0_conv_bi": _L0_conv_in["bi"],
        "L0_conv_Wl": _L0_conv_in["Wl"],
        "L0_conv_bl": _L0_conv_in["bl"],
        "L0_conv_Wg": _L0_conv_in["Wg"],
        "L0_conv_bg": _L0_conv_in["bg"],
        "L0_conv_Wo": _L0_conv_in["Wo"],
        "L0_conv_bo": _L0_conv_in["bo"],
        "L0_conv_gamma": _L0_conv_in["gamma"],
        "L0_conv_beta": _L0_conv_in["beta"],
        "L1_conv_Wi": _L1_conv_in["Wi"],
        "L1_conv_bi": _L1_conv_in["bi"],
        "L1_conv_Wl": _L1_conv_in["Wl"],
        "L1_conv_bl": _L1_conv_in["bl"],
        "L1_conv_Wg": _L1_conv_in["Wg"],
        "L1_conv_bg": _L1_conv_in["bg"],
        "L1_conv_Wo": _L1_conv_in["Wo"],
        "L1_conv_bo": _L1_conv_in["bo"],
        "L1_conv_gamma": _L1_conv_in["gamma"],
        "L1_conv_beta": _L1_conv_in["beta"],
    }

def reference(x, L0_conv_Wi, L0_conv_bi, L0_conv_Wl, L0_conv_bl, L0_conv_Wg, L0_conv_bg, L0_conv_Wo, L0_conv_bo, L0_conv_gamma, L0_conv_beta, L1_conv_Wi, L1_conv_bi, L1_conv_Wl, L1_conv_bl, L1_conv_Wg, L1_conv_bg, L1_conv_Wo, L1_conv_bo, L1_conv_gamma, L1_conv_beta):
    import jax
    import jax.numpy as jnp
    def _L0_conv_ref(x, Wi, bi, Wl, bl, Wg, bg, Wo, bo, gamma, beta, lower_bound):
        import jax, jax.numpy as jnp
        import numpy as np
        H, W, B, D = (64, 64, 16, 256)

        def _scan(inp, lam, axis):

            def combine(a, b):
                la, ia = a
                lb, ib = b
                return (la * lb, lb * ia + ib)
            return jax.lax.associative_scan(combine, (lam, inp), axis=axis)[1]

        def _bidir(inp, lam, axis):
            fwd = _scan(inp, lam, axis)
            rev = jnp.flip(_scan(jnp.flip(inp, axis), jnp.flip(lam, axis), axis), axis)
            return fwd + rev
        lb = jnp.float32(lower_bound)
        inp = jax.nn.silu(x @ Wi + bi)
        gate = jax.nn.silu(x @ Wg + bg)
        lam = lb + (1.0 - lb) * jax.nn.sigmoid(x @ Wl + bl)
        inp = (1.0 - lam) * inp
        hiddens = _bidir(inp, lam, 0) + _bidir(inp, lam, 1)
        mu = jnp.mean(hiddens, axis=-1, keepdims=True)
        var = jnp.mean(jnp.square(hiddens - mu), axis=-1, keepdims=True)
        feat = (hiddens - mu) * jax.lax.rsqrt(var + 1e-05) * gamma + beta
        return feat * gate @ Wo + bo

    def _L1_conv_ref(x, Wi, bi, Wl, bl, Wg, bg, Wo, bo, gamma, beta, lower_bound):
        import jax, jax.numpy as jnp
        import numpy as np
        H, W, B, D = (64, 64, 16, 256)

        def _scan(inp, lam, axis):

            def combine(a, b):
                la, ia = a
                lb, ib = b
                return (la * lb, lb * ia + ib)
            return jax.lax.associative_scan(combine, (lam, inp), axis=axis)[1]

        def _bidir(inp, lam, axis):
            fwd = _scan(inp, lam, axis)
            rev = jnp.flip(_scan(jnp.flip(inp, axis), jnp.flip(lam, axis), axis), axis)
            return fwd + rev
        lb = jnp.float32(lower_bound)
        inp = jax.nn.silu(x @ Wi + bi)
        gate = jax.nn.silu(x @ Wg + bg)
        lam = lb + (1.0 - lb) * jax.nn.sigmoid(x @ Wl + bl)
        inp = (1.0 - lam) * inp
        hiddens = _bidir(inp, lam, 0) + _bidir(inp, lam, 1)
        mu = jnp.mean(hiddens, axis=-1, keepdims=True)
        var = jnp.mean(jnp.square(hiddens - mu), axis=-1, keepdims=True)
        feat = (hiddens - mu) * jax.lax.rsqrt(var + 1e-05) * gamma + beta
        return feat * gate @ Wo + bo

    def _gn(v, G=32, eps=1e-5):
        B_, H_, W_, C_ = v.shape
        g = v.reshape(B_, H_, W_, G, C_ // G)
        m = jnp.mean(g, axis=(1, 2, 4), keepdims=True)
        s = jnp.var(g, axis=(1, 2, 4), keepdims=True)
        return ((g - m) / jnp.sqrt(s + eps)).reshape(v.shape)

    def _ln_c(v, eps=1e-6):
        m = jnp.mean(v, axis=-1, keepdims=True)
        s = jnp.var(v, axis=-1, keepdims=True)
        return (v - m) / jnp.sqrt(s + eps)

    def _ln_t(v, eps=1e-5):
        m = jnp.mean(v, axis=-1, keepdims=True)
        s = jnp.var(v, axis=-1, keepdims=True)
        return (v - m) / jnp.sqrt(s + eps)

    def _to_tokens(v):
        B_, H_, W_, C_ = v.shape
        return v.reshape(B_, H_ * W_, C_)
    def _from_tokens(t, like):
        return t.reshape(like.shape)

    x = x + _L0_conv_ref(_gn(x), L0_conv_Wi, L0_conv_bi, L0_conv_Wl, L0_conv_bl, L0_conv_Wg, L0_conv_bg, L0_conv_Wo, L0_conv_bo, L0_conv_gamma, L0_conv_beta, 0)
    x = x + _L1_conv_ref(_gn(x), L1_conv_Wi, L1_conv_bi, L1_conv_Wl, L1_conv_bl, L1_conv_Wg, L1_conv_bg, L1_conv_Wo, L1_conv_bo, L1_conv_gamma, L1_conv_beta, 0)
    return x


_drawn_inputs = setup_inputs


def setup_inputs(seed=0):
    import zlib

    import numpy as np

    out = dict(_drawn_inputs(seed))
    spreads = {'L0_conv_gamma': (1.0, 0.2),
     'L0_conv_beta': (0.0, 0.458),
     'L1_conv_gamma': (1.0, 0.2),
     'L1_conv_beta': (0.0, 0.462)}
    factors = {'L0_conv_bl': 8.0,
     'L0_conv_bg': 4.674,
     'L1_conv_bi': 2.836,
     'L1_conv_bl': 8.0,
     'L1_conv_bg': 4.916}
    for name, (base, spread) in spreads.items():
        noise = np.random.default_rng([zlib.crc32(name.encode()), seed]).standard_normal(out[name].shape)
        drawn = base * np.exp(spread * noise) if base else spread * noise
        out[name] = jnp.asarray(drawn.astype(out[name].dtype))
    for name, factor in factors.items():
        out[name] = (out[name] * factor).astype(out[name].dtype)
    return out
```

```python
from contextlib import ExitStack

import concourse.bass as bass
from concourse import mybir

F32 = mybir.dt.float32
ALU = mybir.AluOpType
ACT = mybir.ActivationFunctionType
AX_X = mybir.AxisListType.X

P = 128
H, W, NB, D = 64, 64, 16, 256
M = D // P
TOK = H * W
CH = 512
NCH = TOK // CH
HC = CH // W
TT = CH // P
LAYERS = 2
GROUP = 8
GN_EPS, LN_EPS = 1e-5, 1e-5

SB = 8
NBG = NB // SB
UNITS = M * NBG
PARTS = NBG * 2

FILLS = 2 * 3 * NCH
FIRST = 3 * NCH
ROWS = H * M
ROWS_CH = HC * M
SCAN_STEPS = 9


def build(nc, x, w_g, w_i, w_l, w_o, vecs, ident_d, gmat_d, out):
    with ExitStack() as ctx:
        def sb(name, shape):
            return ctx.enter_context(nc.sbuf_tensor(name, shape, F32))

        def sem(name):
            return ctx.enter_context(nc.semaphore(name))

        xn = sb("xn", [P, 2, M, TOK])
        lam = sb("lam", [P, M, TOK])
        inp = sb("inp", [P, M, TOK])
        hid = sb("hid", [P, M, TOK])
        tmp = sb("tmp", [P, TOK])
        wg, wi, wl, wo = (sb(f"w{n}", [P, M, D]) for n in "gilo")
        vec = sb("vec", [P, 6, M])
        ident = sb("ident", [P, P])
        gmat = sb("gmat", [P, P])
        gscale = sb("gscale", [P, M, H])
        gshift = sb("gshift", [P, M, H])
        gate_out = sb("gate_out", [P, 2, CH])
        gate_even = sb("gate_even", [P, M, CH])
        res = sb("res", [P, 2, M, CH])
        lam0 = sb("lam0", [P, H])
        st = sb("st", [P, 2, TT, 6])
        mv = sb("mv", [P, 2, 6, TT])
        ln = sb("ln", [P, 2, 3, TT])
        mone = sb("mone", [P, TT])
        mhalf = sb("mhalf", [P, ROWS])

        ntok = tmp[:, 0:TT * D].rearrange("p (t c) -> p t c", t=TT)
        feat = tmp[:, 1024:3072].rearrange("p (s m n) -> p s m n", s=2, m=M)
        gate_odd = tmp[:, 3072:4096].rearrange("p (m n) -> p m n", m=M)
        gates = [gate_even[:], gate_odd]
        NST = ROWS * NBG * 6
        parts = tmp[:, 0:NST].rearrange("p (m h g s) -> p m h g s", m=M, h=H, g=NBG)
        part = tmp[:, 0:NST].rearrange("p (r k s) -> p r k s", r=ROWS, k=PARTS)
        dev = tmp[:, NST:NST + ROWS * PARTS].rearrange("p (r k) -> p r k", r=ROWS)
        at = NST + ROWS * PARTS
        gsum, gmean, gdev, gm2, gq, gvar = (tmp[:, at + i * ROWS:at + (i + 1) * ROWS] for i in range(6))
        slots = xn[:].rearrange("p s m n -> p (s m) n")

        bank = [ctx.enter_context(nc.psum_tensor(f"bank{i}", [P, 512], F32)) for i in range(8)]
        fill_bank = bank[0:2]
        htok_bank = [bank[2:4], bank[0:2]]
        nchan_bank = bank[4:6]
        out_bank = bank[6:8]

        const_in, weights_in = sem("const_in"), sem("weights_in")
        stat_in = [sem(f"stat_in{i}") for i in range(UNITS)]
        stat_used, gn_sum, gn_mean, gn_link, gn_var, gn_pow, gn_ready = map(
            sem, ("stat_used", "gn_sum", "gn_mean", "gn_link", "gn_var", "gn_pow", "gn_ready"))
        x_in = [[sem(f"x_in{s}_{q}") for q in range(NCH // 2)] for s in range(2)]
        xn_ready, fill_full, filled = map(sem, ("xn_ready", "fill_full", "filled"))
        gate_stored = [sem(f"gate_stored{i}") for i in range(2)]
        gate_in = [sem(f"gate_in{i}") for i in range(2)]
        res_in = [sem(f"res_in{i}") for i in range(2)]
        out_stored = [sem(f"out_stored{i}") for i in range(2)]
        scan_step, scans_done = sem("scan_step"), sem("scans_done")
        htok_full, bn_step, mv_ready, ln_step, rstd_ready, ntok_ready = map(
            sem, ("htok_full", "bn_step", "mv_ready", "ln_step", "rstd_ready", "ntok_ready"))
        nchan_full, feat_ready, prod_ready, out_full, final_done = map(
            sem, ("nchan_full", "feat_ready", "prod_ready", "out_full", "final_done"))
        half_set = sem("half_set")

        mid = nc.dram_tensor("mid", [NB, D, TOK], F32, kind="Internal").ap()
        gates_d = nc.dram_tensor("gates_d", [2, D, TOK], F32, kind="Internal").ap()
        src, dst = [x, mid], [mid, out]

        block = ctx.enter_context(nc.Block())

        def images(eng, layer, period, last_pair_apart):
            def pair(g, last):
                for p in range(2):
                    period(layer * NB + g * 2 + p, layer * (NB // 2) + g, g * 2 + p, p, last)
            loops = NB // 2 - last_pair_apart
            with eng.Fori(0, loops) as g:
                pair(g, False)
            if last_pair_apart:
                pair(loops, True)


        @block.sync
        def _(sp):
            sp.dma_start(ident[:], ident_d).then_inc(const_in, 16)
            sp.dma_start(gmat[:], gmat_d).then_inc(const_in, 16)

            for layer in range(LAYERS):
                xs, xd = src[layer], dst[layer]

                def image_rows(ap, b, a, n):
                    return ap[b].rearrange("(m p) t -> p m t", p=P)[:, :, a:a + n]

                if layer:
                    for s in range(2):
                        sp.wait_ge(out_stored[s], 16 * (NCH // 2) * NB * layer)
                for t, d in ((wg, w_g), (wi, w_i), (wl, w_l), (wo, w_o)):
                    sp.dma_start(t[:], d[layer].rearrange("(k p) n -> p k n", p=P)).then_inc(weights_in, 16)
                sp.dma_start(vec[:], vecs[layer]).then_inc(weights_in, 16)

                def stat_units(hc, again):
                    for u in range(UNITS):
                        m, bg = u // NBG, u % NBG
                        if again:
                            sp.wait_ge(stat_used, UNITS * (NCH * layer) + UNITS * hc - UNITS + u + 1)
                        rows = xs.rearrange("(g b) (m p) (c n) -> g m p b c n", g=NBG, m=M, c=NCH)[bg, m]
                        sp.dma_start(slots[:, u].rearrange("p (b n) -> p b n", b=SB),
                                     rows[:, :, hc]).then_inc(stat_in[u], 16)
                stat_units(0, False)
                with sp.Fori(1, NCH) as hc:
                    stat_units(hc, True)
                sp.wait_ge(stat_used, UNITS * NCH * (layer + 1))

                def load_x(b, p, q):
                    sp.dma_start(xn[:, p, :, 2 * q * CH:2 * (q + 1) * CH],
                                 image_rows(xs, b, 2 * q * CH, 2 * CH)).then_inc(x_in[p][q], 16)

                def load_res(b, j):
                    sp.dma_start(res[:, j % 2], image_rows(xs, b, j * CH, CH)).then_inc(res_in[j % 2], 16)

                def store_gates(p, m, group):
                    for j in range(NCH):
                        sp.wait_ge(filled, group + j + 1)
                        sp.dma_start(gates_d[p, m * P:(m + 1) * P, j * CH:(j + 1) * CH],
                                     gate_out[:, j % 2]).then_inc(gate_stored[j % 2], 16)

                def load_gate(p, j):
                    sp.dma_start(gates[j % 2], image_rows(gates_d, p, j * CH, CH)).then_inc(gate_in[j % 2], 16)

                for b in range(2):
                    for q in range(NCH // 2):
                        load_x(b, b, q)
                store_gates(0, 0, FIRST + FILLS * NB * layer - NCH)
                for j in range(2):
                    load_res(0, j)

                def period(B, half_B, b, p, last):
                    group = B * FILLS + FIRST
                    store_gates(p, 1, group)
                    if not last:
                        for q in range(NCH // 2):
                            sp.wait_ge(fill_full, group + 2 * NCH + 2 * q + 2)
                            load_x(b + 2, p, q)
                    for s in range(2):
                        sp.wait_ge(gate_stored[s], B * (16 * NCH) + 16 * NCH)
                    load_gate(p, 0)
                    if not (last and p):
                        store_gates(1 - p, 0, group + FIRST + 2 * NCH)
                    sp.wait_ge(scans_done, B * 2 + 3)
                    load_gate(p, 1)
                    for j in range(NCH + 1):
                        if j < NCH - 2:
                            sp.wait_ge(prod_ready, B * (2 * NCH) + 2 * j + 2)
                            load_gate(p, j + 2)
                        if j:
                            k = j - 1
                            sp.wait_ge(final_done, B * (2 * NCH) + 2 * k + 2)
                            sp.dma_start(image_rows(xd, b, k * CH, CH), res[:, k % 2]).then_inc(out_stored[k % 2], 16)
                            if k < NCH - 2 or not (last and p):
                                sp.wait_ge(out_stored[k % 2], B * (8 * NCH) + 16 * (k // 2) + 16)
                                if k < NCH - 2:
                                    load_res(b, k + 2)
                                else:
                                    load_res(b + 1, k + 2 - NCH)

                images(sp, layer, period, 1)

            for s in range(2):
                sp.wait_ge(out_stored[s], 16 * (NCH // 2) * NB * LAYERS)
                sp.wait_ge(gate_stored[s], 16 * NCH * NB * LAYERS)

        @block.tensor
        def _(pe):
            pe.wait_ge(const_in, 32)

            def fill(w, m, p, group, first=None):
                for j in range(NCH):
                    if first is not None:
                        pe.wait_ge(xn_ready, first + j + 1)
                    if not isinstance(group, int) or group + j >= 2:
                        pe.wait_ge(filled, group + j - 1)
                    for k in range(M):
                        last = nc.tensor.matmul(fill_bank[j % 2][:], w[:, k, m * P:(m + 1) * P],
                                                xn[:, p, k, j * CH:(j + 1) * CH], start=(k == 0), stop=(k == M - 1))
                    last.then_inc(fill_full, 1)

            for layer in range(LAYERS):
                pe.wait_ge(gn_sum, 2 * layer + 1)
                nc.tensor.matmul(bank[2][:, 0:ROWS], gmat[:], gsum, start=True, stop=True).then_inc(gn_mean, 1)
                pe.wait_ge(gn_sum, 2 * layer + 2)
                nc.tensor.matmul(bank[3][:, 0:ROWS], gmat[:], gq, start=True, stop=True).then_inc(gn_mean, 1)

                pe.wait_ge(weights_in, 80 * (layer + 1))
                group = FIRST + FILLS * NB * layer - FIRST
                fill(wl, 0, 0, group, NCH * NB * layer)
                fill(wi, 0, 0, group + NCH)
                fill(wg, 0, 0, group + 2 * NCH)

                def to_tokens(B, j):
                    for t in range(TT):
                        a = j * CH + t * P
                        for m in range(M):
                            last = nc.tensor.transpose(
                                htok_bank[j % 2][t // 2][:, (t % 2) * D + m * P:(t % 2) * D + (m + 1) * P],
                                hid[:, m, a:a + P], ident[:])
                    last.then_inc(htok_full, 1)

                def project(B, j):
                    pe.wait_ge(prod_ready, B * (2 * NCH) + 2 * j + 2)
                    for m in range(M):
                        if j:
                            pe.wait_ge(final_done, B * (2 * NCH) + 2 * j - 2 + m + 1)
                        for k in range(M):
                            last = nc.tensor.matmul(out_bank[m][:], wo[:, k, m * P:(m + 1) * P],
                                                    feat[:, j % 2, k], start=(k == 0), stop=(k == M - 1))
                        last.then_inc(out_full, 1)

                def period(B, half_B, b, p, last):
                    group = B * FILLS + FIRST
                    fill(wg, 1, p, group)
                    fill(wi, 1, p, group + NCH)
                    fill(wl, 1, p, group + 2 * NCH)
                    after = group + 3 * NCH
                    if not (last and p):
                        fill(wl, 0, 1 - p, after, B * NCH + NCH)
                        fill(wi, 0, 1 - p, after + NCH)
                        fill(wg, 0, 1 - p, after + 2 * NCH)
                        after = after + 3 * NCH
                    pe.wait_ge(scans_done, B * 2 + 3)
                    to_tokens(B, 0)
                    pe.wait_ge(filled, after)
                    to_tokens(B, 1)
                    for j in range(NCH):
                        pe.wait_ge(ntok_ready, B * NCH + j + 1)
                        for m in range(M):
                            for t in range(TT):
                                last_t = nc.tensor.transpose(nchan_bank[m][:, t * P:(t + 1) * P],
                                                             ntok[:, t, m * P:(m + 1) * P], ident[:])
                            last_t.then_inc(nchan_full, 1)
                        if j + 2 < NCH:
                            to_tokens(B, j + 2)
                        if j:
                            project(B, j - 1)
                    project(B, NCH - 1)

                images(pe, layer, period, 1)

        @block.scalar
        def _(act):
            BG, BI, BL, BO, GAMMA, BETA = range(6)

            for layer in range(LAYERS):
                act.wait_ge(weights_in, 80 * (layer + 1))
                act.wait_ge(gn_ready, layer + 1)

                def normalise(B, half_B, p, first, count):
                    for r in range(first, first + count):
                        h, m = r // M, r % M
                        if r % (2 * ROWS_CH) == 0:
                            act.wait_ge(x_in[p][r // (2 * ROWS_CH)], half_B * 16 + 16)
                        row = xn[:, p, m, h * W:(h + 1) * W]
                        ins = nc.scalar.activation(row, row, ACT.Identity, bias=gshift[:, m, h:h + 1],
                                                   scale=gscale[:, m, h:h + 1])
                        if r % ROWS_CH == ROWS_CH - 1:
                            ins.then_inc(xn_ready, 1)

                def evacuate(j, group, func, bias, m, to):
                    act.wait_ge(fill_full, group + j + 1)
                    nc.scalar.activation(to, fill_bank[j % 2][:], func, bias=vec[:, bias, m:m + 1]).then_inc(filled, 1)

                def chunk(t, m, j):
                    return t[:, m, j * CH:(j + 1) * CH]

                def gate_slot(j, stored):
                    if not isinstance(stored, int) or stored + j // 2 > 0:
                        act.wait_ge(gate_stored[j % 2], stored * 16 + 16 * (j // 2))
                    return gate_out[:, j % 2]

                B0 = NB * layer
                normalise(B0, B0 // 2, 0, 0, ROWS)
                group = FILLS * B0
                if layer:
                    act.wait_ge(scans_done, 2 * B0 + 1)
                for j in range(NCH):
                    evacuate(j, group, ACT.Sigmoid, BL, 0, chunk(lam, 0, j))
                    normalise(B0 + 1, B0 // 2, 1, 4 * j, 4)
                for j in range(NCH):
                    evacuate(j, group + NCH, ACT.Silu, BI, 0, chunk(inp, 0, j))
                    normalise(B0 + 1, B0 // 2, 1, 32 + 4 * j, 4)
                for j in range(NCH):
                    evacuate(j, group + 2 * NCH, ACT.Silu, BG, 0, gate_slot(j, B0 * NCH))
                    normalise(B0 + 1, B0 // 2, 1, 64 + 4 * j, 4)

                def period(B, half_B, b, p, last):
                    group = B * FILLS + FIRST
                    nxt = (B + 1, half_B + p, 1 - p)
                    nxt2 = (B + 2, half_B + 1, p)
                    stored = B * NCH + NCH // 2
                    for j in range(NCH):
                        evacuate(j, group, ACT.Silu, BG, 1, gate_slot(j, stored))
                        if not (last and p):
                            normalise(*nxt, 96 + 2 * j, 2)
                    act.wait_ge(scans_done, B * 2 + 1)
                    for j in range(NCH):
                        evacuate(j, group + NCH, ACT.Silu, BI, 1, chunk(inp, 1, j))
                        if not (last and p):
                            normalise(*nxt, 112 + 2 * j, 2)
                    for j in range(NCH):
                        evacuate(j, group + 2 * NCH, ACT.Sigmoid, BL, 1, chunk(lam, 1, j))
                    if not (last and p):
                        act.wait_ge(scans_done, B * 2 + 2)
                        for j in range(NCH):
                            evacuate(j, group + 3 * NCH, ACT.Sigmoid, BL, 0, chunk(lam, 0, j))
                            if not last:
                                normalise(*nxt2, 2 * j, 2)
                        for j in range(NCH):
                            evacuate(j, group + 4 * NCH, ACT.Silu, BI, 0, chunk(inp, 0, j))
                            if not last:
                                normalise(*nxt2, 16 + 2 * j, 2)
                        for j in range(NCH):
                            evacuate(j, group + 5 * NCH, ACT.Silu, BG, 0, gate_slot(j, stored + NCH // 2))
                            if not last:
                                normalise(*nxt2, 32 + 2 * j, 2)

                    def layer_norm(j):
                        act.wait_ge(rstd_ready, B * NCH + j + 1)
                        for t in range(TT):
                            ins = nc.scalar.activation(
                                ntok[:, t], htok_bank[j % 2][t // 2][:, (t % 2) * D:(t % 2 + 1) * D], ACT.Identity,
                                bias=ln[:, j % 2, 2, t:t + 1], scale=ln[:, j % 2, 1, t:t + 1])
                        ins.then_inc(ntok_ready, 1)

                    layer_norm(0)
                    for j in range(NCH):
                        for m in range(M):
                            act.wait_ge(nchan_full, B * (2 * NCH) + 2 * j + m + 1)
                            nc.scalar.activation(feat[:, j % 2, m], nchan_bank[m][:], ACT.Identity,
                                                 bias=vec[:, BETA, m:m + 1],
                                                 scale=vec[:, GAMMA, m:m + 1]).then_inc(feat_ready, 1)
                        if j + 1 < NCH:
                            layer_norm(j + 1)
                        if not last:
                            normalise(*nxt2, 48 + 6 * j, 6)

                images(act, layer, period, 1)

        @block.vector
        def _(dve):
            nc.vector.memset(mone[:], -1.0)
            nc.vector.memset(mhalf[:], -0.5).then_inc(half_set, 1)
            nc.vector.memset(lam0[:], 0.0).then_inc(scans_done, 1)
            gn_at = [0]

            for layer in range(LAYERS):
                with dve.Fori(0, NCH) as hc:
                    for u in range(UNITS):
                        m, bg = u // NBG, u % NBG
                        dve.wait_ge(stat_in[u], hc * 16 + 16 * (NCH * layer + 1))
                        rows = slots[:, u].rearrange("p (b h w) -> p h b w", b=SB, w=W)
                        for h in range(HC):
                            ins = nc.vector.bn_stats(parts[:, m, bass.ds(hc * HC + h, 1), bg].rearrange("p a s -> p (a s)"),
                                                     rows[:, h])
                        ins.then_inc(stat_used, 1)
                dve.wait_ge(stat_used, UNITS * NCH * (layer + 1))

                def link(ins):
                    ins.then_inc(gn_link, 1)
                    gn_at[0] += 1
                    dve.wait_ge(gn_link, gn_at[0])

                mean_k, m2_k = part[:, :, :, 1], part[:, :, :, 2]
                nc.vector.tensor_reduce(gsum, mean_k, AX_X, ALU.add).then_inc(gn_sum, 1)
                dve.wait_ge(gn_mean, 2 * layer + 1)
                link(nc.vector.tensor_copy(gmean, bank[2][:, 0:ROWS]))
                link(nc.vector.tensor_tensor(dev, mean_k, gmean.unsqueeze(2).broadcast_to((P, ROWS, PARTS)),
                                             ALU.subtract))
                link(nc.vector.tensor_tensor(dev, dev, dev, ALU.mult))
                link(nc.vector.tensor_reduce(gdev, dev, AX_X, ALU.add))
                link(nc.vector.tensor_reduce(gm2, m2_k, AX_X, ALU.add))
                nc.vector.scalar_tensor_tensor(out=gq, in0=gm2, scalar=1.0 / (SB * W // 2), in1=gdev, op0=ALU.mult,
                                               op1=ALU.add).then_inc(gn_sum, 1)
                dve.wait_ge(gn_mean, 2 * layer + 2)
                nc.vector.tensor_scalar(gvar, bank[3][:, 0:ROWS], GN_EPS, None, ALU.add).then_inc(gn_var, 1)
                dve.wait_ge(gn_pow, layer + 1)
                nc.vector.scalar_tensor_tensor(out=gshift[:].rearrange("p m h -> p (m h)"), in0=gmean, scalar=-1.0,
                                               in1=gscale[:].rearrange("p m h -> p (m h)"), op0=ALU.mult,
                                               op1=ALU.mult).then_inc(gn_ready, 1)

                def scans(B, m):
                    L, I, S = lam[:, m], inp[:, m], hid[:, m]
                    base = B * (2 * SCAN_STEPS) + m * SCAN_STEPS
                    cols = [t.rearrange("p (h w) -> p w h", w=W) for t in (L, I, S, tmp[:])]
                    Lc, Ic, Sc, Tc = cols
                    dve.wait_ge(filled, B * FILLS + (FIRST - NCH if m == 0 else 2 * FIRST))
                    nc.vector.scalar_tensor_tensor(out=I, in0=L, scalar=1.0, in1=I, op0=ALU.subtract,
                                                   op1=ALU.mult).then_inc(scan_step, 1)
                    dve.wait_ge(scan_step, base + 1)
                    for w in range(W):
                        nc.vector.tensor_tensor_scan(Sc[:, w], Lc[:, w], Ic[:, w], 0.0, ALU.mult, ALU.add)
                    for w in range(W):
                        nc.vector.tensor_tensor_scan(Tc[:, w, ::-1], Lc[:, w, ::-1], Ic[:, w, ::-1], 0.0,
                                                     ALU.mult, ALU.add)
                    nc.vector.tensor_copy(lam0[:], Lc[:, 0]).then_inc(scan_step, 1)
                    dve.wait_ge(scan_step, base + 2)
                    nc.vector.memset(Lc[:, 0], 0.0).then_inc(scan_step, 1)
                    nc.vector.tensor_tensor(S, S, tmp[:], ALU.add).then_inc(scan_step, 1)
                    dve.wait_ge(scan_step, base + 4)
                    nc.vector.tensor_tensor_scan(tmp[:], L, I, 0.0, ALU.mult, ALU.add).then_inc(scan_step, 1)
                    dve.wait_ge(scan_step, base + 5)
                    nc.vector.tensor_copy(Lc[:, 0], lam0[:]).then_inc(scan_step, 1)
                    nc.vector.memset(Lc[:, W - 1], 0.0).then_inc(scan_step, 1)
                    nc.vector.tensor_tensor(S, S, tmp[:], ALU.add).then_inc(scan_step, 1)
                    dve.wait_ge(scan_step, base + 8)
                    nc.vector.tensor_tensor_scan(tmp[:, ::-1], L[:, ::-1], I[:, ::-1], 0.0, ALU.mult,
                                                 ALU.add).then_inc(scan_step, 1)
                    dve.wait_ge(scan_step, base + 9)
                    nc.vector.tensor_tensor(S, S, tmp[:], ALU.add).then_inc(scans_done, 1)

                def period(B, half_B, b, p, last):
                    for m in range(M):
                        scans(B, m)

                    def statistics(j):
                        s = j % 2
                        dve.wait_ge(htok_full, B * NCH + j + 1)
                        for t in range(TT):
                            ins = nc.vector.bn_stats(st[:, s, t], htok_bank[s][t // 2][:, (t % 2) * D:(t % 2 + 1) * D])
                        ins.then_inc(bn_step, 1)
                        at = B * (3 * NCH) + 3 * j
                        dve.wait_ge(bn_step, at + 1)
                        _, mean_e, m2_e, _, mean_o, m2_o = (st[:, s, :, i] for i in range(6))
                        total, diff, m2, mean, dsq, var = (mv[:, s, i] for i in range(6))
                        nc.vector.tensor_tensor(total, mean_e, mean_o, ALU.add)
                        nc.vector.tensor_tensor(diff, mean_e, mean_o, ALU.subtract)
                        nc.vector.scalar_tensor_tensor(out=m2, in0=m2_e, scalar=D * LN_EPS, in1=m2_o, op0=ALU.add,
                                                       op1=ALU.add).then_inc(bn_step, 1)
                        dve.wait_ge(bn_step, at + 2)
                        nc.vector.tensor_scalar(mean, total, 0.5, None, ALU.mult)
                        nc.vector.scalar_tensor_tensor(out=dsq, in0=diff, scalar=0.25, in1=diff, op0=ALU.mult,
                                                       op1=ALU.mult).then_inc(bn_step, 1)
                        dve.wait_ge(bn_step, at + 3)
                        nc.vector.scalar_tensor_tensor(out=var, in0=m2, scalar=1.0 / D, in1=dsq, op0=ALU.mult,
                                                       op1=ALU.add).then_inc(mv_ready, 1)

                    def final(j):
                        dve.wait_ge(res_in[j % 2], B * (8 * NCH) + 16 * (j // 2) + 16)
                        for m in range(M):
                            dve.wait_ge(out_full, B * (2 * NCH) + 2 * j + m + 1)
                            nc.vector.scalar_tensor_tensor(out=res[:, j % 2, m], in0=out_bank[m][:],
                                                           scalar=vec[:, 3, m:m + 1], in1=res[:, j % 2, m],
                                                           op0=ALU.add, op1=ALU.add).then_inc(final_done, 1)

                    dve.wait_ge(scans_done, B * 2 + 3)
                    statistics(0)
                    statistics(1)
                    for j in range(NCH):
                        dve.wait_ge(gate_in[j % 2], B * (8 * NCH) + 16 * (j // 2) + 16)
                        for m in range(M):
                            dve.wait_ge(feat_ready, B * (2 * NCH) + 2 * j + m + 1)
                            nc.vector.tensor_tensor(feat[:, j % 2, m], feat[:, j % 2, m], gates[j % 2][:, m],
                                                    ALU.mult).then_inc(prod_ready, 1)
                        if j + 2 < NCH:
                            statistics(j + 2)
                        if j:
                            final(j - 1)
                    final(NCH - 1)

                images(dve, layer, period, 0)

        @block.gpsimd
        def _(pool):
            pool.wait_ge(half_set, 1)
            for layer in range(LAYERS):
                pool.wait_ge(gn_var, layer + 1)
                nc.gpsimd.tensor_tensor(gscale[:].rearrange("p m h -> p (m h)"), gvar, mhalf[:],
                                        ALU.pow).then_inc(gn_pow, 1)

                def period(B, half_B, b, p, last):
                    for j in range(NCH):
                        s = j % 2
                        mean, var = mv[:, s, 3], mv[:, s, 5]
                        rstd, neg, shift = (ln[:, s, i] for i in range(3))
                        pool.wait_ge(mv_ready, B * NCH + j + 1)
                        nc.gpsimd.tensor_tensor(rstd, var, mhalf[:, 0:TT], ALU.pow).then_inc(ln_step, 1)
                        pool.wait_ge(ln_step, B * NCH + j + 1)
                        nc.gpsimd.tensor_tensor(neg, rstd, mone[:], ALU.mult)
                        nc.gpsimd.tensor_tensor(shift, mean, rstd, ALU.mult).then_inc(rstd_ready, 1)

                images(pool, layer, period, 0)


_WEIGHTS = ("Wg", "Wi", "Wl", "Wo")
_VECTORS = ("bg", "bi", "bl", "bo", "gamma", "beta")


def kernel(**inputs):
    import numpy as np
    import concourse.bacc as bacc
    from concourse.bass_utils import run_bass_kernel_spmd

    nc = bacc.Bacc("TRN2", target_bir_lowering=False, num_devices=1)
    arrays = {}

    def give(name, a):
        a = np.ascontiguousarray(a)
        arrays[name] = a
        return nc.dram_tensor(name, a.shape, mybir.dt.from_np(a.dtype), kind="ExternalInput").ap()

    x = give("x_cm", np.asarray(inputs["x"]).transpose(2, 3, 0, 1).reshape(NB, D, TOK))
    ws = [[give(f"w{layer}_{n}", np.asarray(inputs[f"L{layer}_conv_{n}"])) for layer in range(LAYERS)]
          for n in _WEIGHTS]
    vecs = [give(f"vecs{layer}", np.stack([np.asarray(inputs[f"L{layer}_conv_{n}"]).reshape(M, P)
                                           for n in _VECTORS]).transpose(2, 0, 1)) for layer in range(LAYERS)]
    ident = give("ident_c", np.eye(P, dtype=np.float32))
    gmat = give("gmat_c", np.kron(np.eye(P // GROUP), np.full((GROUP, GROUP), 1.0 / (GROUP * PARTS))).astype(np.float32))
    out = nc.dram_tensor("out_cm", (NB, D, TOK), F32, kind="ExternalOutput").ap()
    build(nc, x, *ws, vecs, ident, gmat, out)
    r = run_bass_kernel_spmd(nc, [arrays], core_ids=[0])
    y = np.asarray(r.results[0]["out_cm"])
    return np.ascontiguousarray(y.reshape(NB, D, H, W).transpose(2, 3, 0, 1))
```

```python
from contextlib import ExitStack

import concourse.bass as bass
from concourse import mybir

F32 = mybir.dt.float32
ALU = mybir.AluOpType
ACT = mybir.ActivationFunctionType
AX_X = mybir.AxisListType.X

P = 128
H, W, NB, D = 64, 64, 16, 256
M = D // P
TOK = H * W
CH = 512
NCH = TOK // CH
HC = CH // W
TT = CH // P
LAYERS = 2
GROUP = 8
GN_EPS, LN_EPS = 1e-5, 1e-5

SB = 8
NBG = NB // SB
UNITS = M * NBG
PARTS = NBG * 2

FILLS = 2 * 3 * NCH
FIRST = 2 * NCH
ROWS = H * M
ROWS_CH = HC * M
SCAN_STEPS = 9
STORED = 16 * M
L1, I1, G, I0, L0 = 0, NCH, 2 * NCH, 4 * NCH, 5 * NCH
BG, BI, BL, BO, GAMMA, BETA = range(6)
EARLY = 2 * ROWS_CH
LATE = 4


def first_fills(inp, lam):
    return [(inp, j) for j in range(NCH // 2)] + [(lam, j) for j in range(NCH)] + \
           [(inp, j) for j in range(NCH // 2, NCH)]


def first_by_dve(h, m):
    return m == 0 or h % 2 == 0


def build(nc, x, w_g, w_i, w_l, w_o, vecs, ident_d, gmat_d, out):
    with ExitStack() as ctx:
        def sb(name, shape):
            return ctx.enter_context(nc.sbuf_tensor(name, shape, F32))

        def sem(name):
            return ctx.enter_context(nc.semaphore(name))

        xn = sb("xn", [P, 2, M, TOK])
        lam = sb("lam", [P, M, TOK])
        inp = sb("inp", [P, M, TOK])
        hid = sb("hid", [P, M, TOK])
        tmp = sb("tmp", [P, TOK])
        wg, wi, wl, wo = (sb(f"w{n}", [P, M, D]) for n in "gilo")
        vec = sb("vec", [P, 6, M])
        ident = sb("ident", [P, P])
        gmat = sb("gmat", [P, P])
        gscale = sb("gscale", [P, M, H])
        gshift = sb("gshift", [P, M, H])
        ntok = sb("ntok", [P, TT, D])
        feat = sb("feat", [P, 2, M, CH])
        lam0 = sb("lam0", [P, H])
        st = sb("st", [P, 2, TT, 6])
        mv = sb("mv", [P, 2, 6, TT])
        ln = sb("ln", [P, 2, 3, TT])
        mone = sb("mone", [P, TT])
        mhalf = sb("mhalf", [P, ROWS])

        res = [lam[:, 1], inp[:, 1]]
        NST = ROWS * NBG * 6
        parts = tmp[:, 0:NST].rearrange("p (m h g s) -> p m h g s", m=M, h=H, g=NBG)
        part = tmp[:, 0:NST].rearrange("p (r k s) -> p r k s", r=ROWS, k=PARTS)
        dev = tmp[:, NST:NST + ROWS * PARTS].rearrange("p (r k) -> p r k", r=ROWS)
        at = NST + ROWS * PARTS
        gsum, gmean, gdev, gm2, gq, gvar = (tmp[:, at + i * ROWS:at + (i + 1) * ROWS] for i in range(6))

        def per_row(t):
            return t.rearrange("p (m h) -> p m h", m=M)

        slots = xn[:].rearrange("p s m n -> p (s m) n")

        bank = [ctx.enter_context(nc.psum_tensor(f"bank{i}", [P, 512], F32)) for i in range(8)]
        fill_bank = bank[0:2]
        gate_bank = [bank[0:2], bank[6:8]]
        nchan_bank = bank[4:6]
        out_bank = bank[6:8]

        def htok_bank(j):
            return bank[2:4] if j % 2 == 0 else out_bank if j == 1 else fill_bank

        const_in, weights_in = sem("const_in"), sem("weights_in")
        stat_in = [sem(f"stat_in{i}") for i in range(UNITS)]
        stat_used, gn_sum, gn_mean, gn_link, gn_var, gn_pow, gn_ready = map(
            sem, ("stat_used", "gn_sum", "gn_mean", "gn_link", "gn_var", "gn_pow", "gn_ready"))
        x_in = [[sem(f"x_in{s}_{q}") for q in range(NCH // 2)] for s in range(2)]
        xn_ready, xn0_ready, fill_full, filled = map(sem, ("xn_ready", "xn0_ready", "fill_full", "filled"))
        res_in = [sem(f"res_in{i}") for i in range(NCH // 2)]
        out_stored = [sem(f"out_stored{i}") for i in range(NCH // 2)]
        scan_step, scans_done = sem("scan_step"), sem("scans_done")
        htok_full, bn_step, mv_ready, ln_step, rstd_ready, ntok_ready = map(
            sem, ("htok_full", "bn_step", "mv_ready", "ln_step", "rstd_ready", "ntok_ready"))
        nchan_full, feat_ready, prod_ready, out_full, final_done = map(
            sem, ("nchan_full", "feat_ready", "prod_ready", "out_full", "final_done"))
        half_set = sem("half_set")

        mid = nc.dram_tensor("mid", [NB, D, TOK], F32, kind="Internal").ap()
        src, dst = [x, mid], [mid, out]

        block = ctx.enter_context(nc.Block())

        def images(eng, layer, period, last_pair_apart):
            def pair(g, last):
                for p in range(2):
                    period(layer * NB + g * 2 + p, layer * (NB // 2) + g, g * 2 + p, p, last)
            loops = NB // 2 - last_pair_apart
            with eng.Fori(0, loops) as g:
                pair(g, False)
            if last_pair_apart:
                pair(loops, True)


        @block.sync
        def _(sp):
            sp.dma_start(ident[:], ident_d).then_inc(const_in, 16)
            sp.dma_start(gmat[:], gmat_d).then_inc(const_in, 16)

            for layer in range(LAYERS):
                xs, xd = src[layer], dst[layer]

                def image_rows(ap, b, a, n):
                    return ap[b].rearrange("(m p) t -> p m t", p=P)[:, :, a:a + n]

                if layer:
                    for q in range(NCH // 2):
                        sp.wait_ge(out_stored[q], 16 + STORED * NB * layer)
                for t, d in ((wg, w_g), (wi, w_i), (wl, w_l), (wo, w_o)):
                    sp.dma_start(t[:], d[layer].rearrange("(k p) n -> p k n", p=P)).then_inc(weights_in, 16)
                sp.dma_start(vec[:], vecs[layer]).then_inc(weights_in, 16)

                def stat_units(hc, again):
                    for u in range(UNITS):
                        m, bg = u // NBG, u % NBG
                        if again:
                            sp.wait_ge(stat_used, UNITS * (NCH * layer) + UNITS * hc - UNITS + u + 1)
                        rows = xs.rearrange("(g b) (m p) (c n) -> g m p b c n", g=NBG, m=M, c=NCH)[bg, m]
                        sp.dma_start(slots[:, u].rearrange("p (b n) -> p b n", b=SB),
                                     rows[:, :, hc]).then_inc(stat_in[u], 16)
                stat_units(0, False)
                with sp.Fori(1, NCH) as hc:
                    stat_units(hc, True)
                sp.wait_ge(stat_used, UNITS * NCH * (layer + 1))

                def load_x(b, p, q):
                    sp.dma_start(xn[:, p, :, 2 * q * CH:2 * (q + 1) * CH],
                                 image_rows(xs, b, 2 * q * CH, 2 * CH)).then_inc(x_in[p][q], 16)

                def res_rows(ap, b, m, q):
                    return ap[b, m * P:(m + 1) * P, 2 * q * CH:2 * (q + 1) * CH]

                for b in range(2):
                    for q in range(NCH // 2):
                        load_x(b, b, q)

                def period(B, half_B, b, p, last):
                    sp.wait_ge(scans_done, B * 2 + 3)
                    for q in range(NCH // 2):
                        for m in range(M):
                            sp.dma_start(res[m][:, 2 * q * CH:2 * (q + 1) * CH],
                                         res_rows(xs, b, m, q)).then_inc(res_in[q], 16)
                    for q in range(NCH // 2):
                        sp.wait_ge(final_done, B * (2 * NCH) + 4 * q + 4)
                        for m in range(M):
                            sp.dma_start(res_rows(xd, b, m, q),
                                         res[m][:, 2 * q * CH:2 * (q + 1) * CH]).then_inc(out_stored[q], 16)
                        if not last:
                            load_x(b + 2, p, q)

                images(sp, layer, period, 1)

            for q in range(NCH // 2):
                sp.wait_ge(out_stored[q], 16 + STORED * NB * LAYERS)

        @block.tensor
        def _(pe):
            pe.wait_ge(const_in, 32)

            def project_in(w, m, p, j, to):
                for k in range(M):
                    last = nc.tensor.matmul(to[:], w[:, k, m * P:(m + 1) * P],
                                            xn[:, p, k, j * CH:(j + 1) * CH], start=(k == 0), stop=(k == M - 1))
                last.then_inc(fill_full, 1)

            def fill(w, m, p, group, normed=None, first=0, end=NCH):
                for j in range(first, end):
                    if normed is not None:
                        pe.wait_ge(xn_ready, normed + j + 1)
                    pe.wait_ge(filled, group + j - 1)
                    project_in(w, m, p, j, fill_bank[j % 2])

            def fill_gates(p, group):
                for j in range(NCH):
                    for m in range(M):
                        if j == 0:
                            pe.wait_ge(filled, group - 1 + m)
                        elif j > 1:
                            pe.wait_ge(filled, group + 2 * (j - 2) + m + 1)
                        project_in(wg, m, p, j, gate_bank[j % 2][m])

            for layer in range(LAYERS):
                pe.wait_ge(gn_sum, 2 * layer + 1)
                nc.tensor.matmul(bank[2][:, 0:ROWS], gmat[:], gsum, start=True, stop=True).then_inc(gn_mean, 1)
                pe.wait_ge(gn_sum, 2 * layer + 2)
                nc.tensor.matmul(bank[3][:, 0:ROWS], gmat[:], gq, start=True, stop=True).then_inc(gn_mean, 1)

                pe.wait_ge(weights_in, 80 * (layer + 1))
                group = FILLS * NB * layer
                for g, (w, j) in enumerate(first_fills(wi, wl)):
                    pe.wait_ge(xn0_ready, NCH * layer + j + 1)
                    pe.wait_ge(xn_ready, NCH * NB * layer + j + 1)
                    if group + g > 1:
                        pe.wait_ge(filled, group + g - 1)
                    project_in(w, 0, 0, j, fill_bank[g % 2])

                def to_tokens(B, j):
                    for t in range(TT):
                        a = j * CH + t * P
                        for m in range(M):
                            last = nc.tensor.transpose(
                                htok_bank(j)[t // 2][:, (t % 2) * D + m * P:(t % 2) * D + (m + 1) * P],
                                hid[:, m, a:a + P], ident[:])
                    last.then_inc(htok_full, 1)

                def project(B, j):
                    pe.wait_ge(prod_ready, B * (2 * NCH) + 2 * j + 2)
                    for m in range(M):
                        if j:
                            pe.wait_ge(final_done, B * (2 * NCH) + 2 * j - 2 + m + 1)
                        for k in range(M):
                            last = nc.tensor.matmul(out_bank[m][:], wo[:, k, m * P:(m + 1) * P],
                                                    feat[:, j % 2, k], start=(k == 0), stop=(k == M - 1))
                        last.then_inc(out_full, 1)

                def period(B, half_B, b, p, last):
                    group = B * FILLS + FIRST
                    has_next = not (last and p)
                    fill(wl, 1, p, group + L1)
                    fill(wi, 1, p, group + I1)
                    fill_gates(p, group + G)
                    if has_next:
                        fill(wi, 0, 1 - p, group + I0, B * NCH + NCH)
                        fill(wl, 0, 1 - p, group + L0, end=NCH - LATE)
                    pe.wait_ge(scans_done, B * 2 + 3)
                    pe.wait_ge(filled, group + I0)
                    to_tokens(B, 0)
                    to_tokens(B, 1)
                    if has_next:
                        fill(wl, 0, 1 - p, group + L0, first=NCH - LATE)
                    for j in range(NCH):
                        pe.wait_ge(ntok_ready, B * NCH + j + 1)
                        for m in range(M):
                            for t in range(TT):
                                last_t = nc.tensor.transpose(nchan_bank[m][:, t * P:(t + 1) * P],
                                                             ntok[:, t, m * P:(m + 1) * P], ident[:])
                            last_t.then_inc(nchan_full, 1)
                        if j + 2 < NCH:
                            if j == 1:
                                pe.wait_ge(filled, group + (FILLS if has_next else FILLS - FIRST))
                            to_tokens(B, j + 2)
                        if j:
                            project(B, j - 1)
                    project(B, NCH - 1)

                images(pe, layer, period, 1)

        @block.scalar
        def _(act):
            for layer in range(LAYERS):
                act.wait_ge(weights_in, 80 * (layer + 1))

                def normalise(half_B, p, first, count, is_first=False):
                    for r in range(first, first + count):
                        h, m = r // M, r % M
                        if r % (2 * ROWS_CH) == 0:
                            act.wait_ge(x_in[p][r // (2 * ROWS_CH)], half_B * 16 + 16)
                        if is_first:
                            if r % ROWS_CH == 0:
                                act.wait_ge(gn_ready, NCH * layer + h // HC + 1)
                            if first_by_dve(h, m):
                                continue
                        row = xn[:, p, m, h * W:(h + 1) * W]
                        ins = nc.scalar.activation(row, row, ACT.Identity, bias=gshift[:, m, h:h + 1],
                                                   scale=gscale[:, m, h:h + 1])
                        if r % ROWS_CH == ROWS_CH - 1:
                            ins.then_inc(xn_ready, 1)

                def evacuate(j, group, func, bias, m, to):
                    act.wait_ge(fill_full, group + j + 1)
                    nc.scalar.activation(to, fill_bank[j % 2][:], func, bias=vec[:, bias, m:m + 1]).then_inc(filled, 1)

                def chunk(t, m, j):
                    return t[:, m, j * CH:(j + 1) * CH]

                B0 = NB * layer
                normalise(B0 // 2, 0, 0, 2 * ROWS_CH, True)
                for g, (t, j) in enumerate(first_fills(inp, lam)):
                    act.wait_ge(fill_full, FILLS * B0 + g + 1)
                    nc.scalar.activation(chunk(t, 0, j), fill_bank[g % 2][:], ACT.Sigmoid if t is lam else ACT.Silu,
                                         bias=vec[:, BL if t is lam else BI, 0:1]).then_inc(filled, 1)
                    if g + 2 < NCH:
                        normalise(B0 // 2, 0, ROWS_CH * (g + 2), ROWS_CH, True)
                normalise(B0 // 2, 1, 0, EARLY)

                def period(B, half_B, b, p, last):
                    group = B * FILLS + FIRST
                    has_next = not (last and p)
                    rows_done = [EARLY]

                    def normalise_next(count):
                        if has_next:
                            normalise(half_B + p, 1 - p, rows_done[0], count)
                            rows_done[0] += count

                    for j in range(NCH):
                        if j % 2 == 0:
                            act.wait_ge(out_stored[j // 2], B * STORED + 16)
                        evacuate(j, group + L1, ACT.Sigmoid, BL, 1, chunk(lam, 1, j))
                        normalise_next(2)
                    for j in range(NCH):
                        evacuate(j, group + I1, ACT.Silu, BI, 1, chunk(inp, 1, j))
                        normalise_next(3)
                    for j in range(NCH):
                        act.wait_ge(fill_full, group + G + 2 * j + 2)
                        for m in range(M):
                            nc.scalar.activation(xn[:, p, m, j * CH:(j + 1) * CH], gate_bank[j % 2][m][:], ACT.Silu,
                                                 bias=vec[:, BG, m:m + 1]).then_inc(filled, 1)
                        normalise_next(7)
                    if has_next:
                        act.wait_ge(scans_done, B * 2 + 2)
                        for j in range(NCH):
                            evacuate(j, group + I0, ACT.Silu, BI, 0, chunk(inp, 0, j))
                        for j in range(NCH - LATE + 2):
                            evacuate(j, group + L0, ACT.Sigmoid, BL, 0, chunk(lam, 0, j))

                    def layer_norm(j):
                        act.wait_ge(rstd_ready, B * NCH + j + 1)
                        for t in range(TT):
                            ins = nc.scalar.activation(
                                ntok[:, t], htok_bank(j)[t // 2][:, (t % 2) * D:(t % 2 + 1) * D], ACT.Identity,
                                bias=ln[:, j % 2, 2, t:t + 1], scale=ln[:, j % 2, 1, t:t + 1])
                        ins.then_inc(ntok_ready, 1)

                    layer_norm(0)
                    if has_next:
                        for j in range(NCH - LATE + 2, NCH):
                            evacuate(j, group + L0, ACT.Sigmoid, BL, 0, chunk(lam, 0, j))
                    for j in range(NCH):
                        for m in range(M):
                            act.wait_ge(nchan_full, B * (2 * NCH) + 2 * j + m + 1)
                            nc.scalar.activation(feat[:, j % 2, m], nchan_bank[m][:], ACT.Identity,
                                                 bias=vec[:, BETA, m:m + 1],
                                                 scale=vec[:, GAMMA, m:m + 1]).then_inc(feat_ready, 1)
                        if j + 1 < NCH:
                            layer_norm(j + 1)
                        if not last and j == NCH - 3:
                            normalise(half_B + 1, p, 0, ROWS_CH // 2)
                        if not last and j == NCH - 2:
                            normalise(half_B + 1, p, ROWS_CH // 2, ROWS_CH // 2)
                    if not last:
                        normalise(half_B + 1, p, ROWS_CH, EARLY - ROWS_CH)

                images(act, layer, period, 1)

        @block.vector
        def _(dve):
            nc.vector.memset(mone[:], -1.0)
            nc.vector.memset(mhalf[:], -0.5).then_inc(half_set, 1)
            nc.vector.memset(lam0[:], 0.0).then_inc(scans_done, 1)
            for q in range(NCH // 2):
                nc.vector.memset(st[:, 0, q], 0.0).then_inc(out_stored[q], 16)
            gn_at = [0]

            for layer in range(LAYERS):
                with dve.Fori(0, NCH) as hc:
                    for u in range(UNITS):
                        m, bg = u // NBG, u % NBG
                        dve.wait_ge(stat_in[u], hc * 16 + 16 * (NCH * layer + 1))
                        rows = slots[:, u].rearrange("p (b h w) -> p h b w", b=SB, w=W)
                        for h in range(HC):
                            ins = nc.vector.bn_stats(parts[:, m, bass.ds(hc * HC + h, 1), bg].rearrange("p a s -> p (a s)"),
                                                     rows[:, h])
                        ins.then_inc(stat_used, 1)
                dve.wait_ge(stat_used, UNITS * NCH * (layer + 1))

                def link(ins):
                    ins.then_inc(gn_link, 1)
                    gn_at[0] += 1
                    dve.wait_ge(gn_link, gn_at[0])

                mean_k, m2_k = part[:, :, :, 1], part[:, :, :, 2]
                nc.vector.tensor_reduce(gsum, mean_k, AX_X, ALU.add).then_inc(gn_sum, 1)
                dve.wait_ge(gn_mean, 2 * layer + 1)
                link(nc.vector.tensor_copy(gmean, bank[2][:, 0:ROWS]))
                link(nc.vector.tensor_tensor(dev, mean_k, gmean.unsqueeze(2).broadcast_to((P, ROWS, PARTS)),
                                             ALU.subtract))
                link(nc.vector.tensor_tensor(dev, dev, dev, ALU.mult))
                link(nc.vector.tensor_reduce(gdev, dev, AX_X, ALU.add))
                link(nc.vector.tensor_reduce(gm2, m2_k, AX_X, ALU.add))
                nc.vector.scalar_tensor_tensor(out=gq, in0=gm2, scalar=1.0 / (SB * W // 2), in1=gdev, op0=ALU.mult,
                                               op1=ALU.add).then_inc(gn_sum, 1)
                dve.wait_ge(gn_mean, 2 * layer + 2)
                nc.vector.tensor_scalar(gvar, bank[3][:, 0:ROWS], GN_EPS, None, ALU.add).then_inc(gn_var, 1)
                for j in range(NCH):
                    dve.wait_ge(gn_pow, NCH * layer + j + 1)
                    rows = slice(j * HC, (j + 1) * HC)
                    nc.vector.scalar_tensor_tensor(out=gshift[:, :, rows], in0=per_row(gmean)[:, :, rows], scalar=-1.0,
                                                   in1=gscale[:, :, rows], op0=ALU.mult,
                                                   op1=ALU.mult).then_inc(gn_ready, 1)
                    dve.wait_ge(gn_ready, NCH * layer + j + 1)
                    if j % 2 == 0:
                        dve.wait_ge(x_in[0][j // 2], 16 * (NB // 2 * layer + 1))
                    for h in range(j * HC, (j + 1) * HC):
                        for m in range(M):
                            if first_by_dve(h, m):
                                row = xn[:, 0, m, h * W:(h + 1) * W]
                                ins = nc.vector.tensor_scalar(row, row, gscale[:, m, h:h + 1], gshift[:, m, h:h + 1],
                                                              ALU.mult, ALU.add)
                    ins.then_inc(xn0_ready, 1)

                def columns(t):
                    return t.rearrange("p (h w) -> p w h", w=W)

                def scan_input(B, m, part, parts):
                    dve.wait_ge(filled, B * FILLS + (FIRST if m == 0 else FIRST + G) - (parts - 1 - part) * NCH // parts)
                    tokens = slice(part * TOK // parts, (part + 1) * TOK // parts)
                    ins = nc.vector.scalar_tensor_tensor(out=inp[:, m, tokens], in0=lam[:, m, tokens], scalar=1.0,
                                                         in1=inp[:, m, tokens], op0=ALU.subtract, op1=ALU.mult)
                    if part == parts - 1:
                        ins.then_inc(scan_step, 1)
                        dve.wait_ge(scan_step, (B * 2 + m) * SCAN_STEPS + 1)

                def scan_up(m, first, end):
                    Lc, Ic, Tc = (columns(t) for t in (lam[:, m], inp[:, m], tmp[:]))
                    for w in range(first, end):
                        nc.vector.tensor_tensor_scan(Tc[:, w, ::-1], Lc[:, w, ::-1], Ic[:, w, ::-1], 0.0,
                                                     ALU.mult, ALU.add)

                def scans(B, m):
                    L, I, S = lam[:, m], inp[:, m], hid[:, m]
                    base = (B * 2 + m) * SCAN_STEPS
                    Lc, Ic, Sc = (columns(t) for t in (L, I, S))
                    for w in range(W):
                        nc.vector.tensor_tensor_scan(Sc[:, w], Lc[:, w], Ic[:, w], 0.0, ALU.mult, ALU.add)
                    nc.vector.tensor_copy(lam0[:], Lc[:, 0]).then_inc(scan_step, 1)
                    dve.wait_ge(scan_step, base + 2)
                    nc.vector.memset(Lc[:, 0], 0.0).then_inc(scan_step, 1)
                    nc.vector.tensor_tensor(S, S, tmp[:], ALU.add).then_inc(scan_step, 1)
                    dve.wait_ge(scan_step, base + 4)
                    nc.vector.tensor_tensor_scan(tmp[:], L, I, 0.0, ALU.mult, ALU.add).then_inc(scan_step, 1)
                    dve.wait_ge(scan_step, base + 5)
                    nc.vector.tensor_copy(Lc[:, 0], lam0[:]).then_inc(scan_step, 1)
                    nc.vector.memset(Lc[:, W - 1], 0.0).then_inc(scan_step, 1)
                    nc.vector.tensor_tensor(S, S, tmp[:], ALU.add).then_inc(scan_step, 1)
                    dve.wait_ge(scan_step, base + 8)
                    nc.vector.tensor_tensor_scan(tmp[:, ::-1], L[:, ::-1], I[:, ::-1], 0.0, ALU.mult,
                                                 ALU.add).then_inc(scan_step, 1)
                    dve.wait_ge(scan_step, base + 9)
                    nc.vector.tensor_tensor(S, S, tmp[:], ALU.add).then_inc(scans_done, 1)

                def period(B, half_B, b, p, last):
                    has_next = not (last and p)
                    scans(B, 0)
                    scan_input(B, 1, 0, 1)
                    dve.wait_ge(scans_done, B * 2 + 2)
                    scan_up(1, 0, W)
                    scans(B, 1)

                    def statistics(j):
                        s = j % 2
                        dve.wait_ge(htok_full, B * NCH + j + 1)
                        for t in range(TT):
                            ins = nc.vector.bn_stats(st[:, s, t], htok_bank(j)[t // 2][:, (t % 2) * D:(t % 2 + 1) * D])
                        ins.then_inc(bn_step, 1)
                        at = B * (3 * NCH) + 3 * j
                        dve.wait_ge(bn_step, at + 1)
                        _, mean_e, m2_e, _, mean_o, m2_o = (st[:, s, :, i] for i in range(6))
                        total, diff, m2, mean, dsq, var = (mv[:, s, i] for i in range(6))
                        nc.vector.tensor_tensor(total, mean_e, mean_o, ALU.add)
                        nc.vector.tensor_tensor(diff, mean_e, mean_o, ALU.subtract)
                        nc.vector.scalar_tensor_tensor(out=m2, in0=m2_e, scalar=D * LN_EPS, in1=m2_o, op0=ALU.add,
                                                       op1=ALU.add).then_inc(bn_step, 1)
                        dve.wait_ge(bn_step, at + 2)
                        nc.vector.tensor_scalar(mean, total, 0.5, None, ALU.mult)
                        nc.vector.scalar_tensor_tensor(out=dsq, in0=diff, scalar=0.25, in1=diff, op0=ALU.mult,
                                                       op1=ALU.mult).then_inc(bn_step, 1)
                        dve.wait_ge(bn_step, at + 3)
                        nc.vector.scalar_tensor_tensor(out=var, in0=m2, scalar=1.0 / D, in1=dsq, op0=ALU.mult,
                                                       op1=ALU.add).then_inc(mv_ready, 1)

                    def final(j):
                        dve.wait_ge(res_in[j // 2], B * 32 + 32)
                        for m in range(M):
                            dve.wait_ge(out_full, B * (2 * NCH) + 2 * j + m + 1)
                            rows = res[m][:, j * CH:(j + 1) * CH]
                            nc.vector.scalar_tensor_tensor(out=rows, in0=out_bank[m][:],
                                                           scalar=vec[:, BO, m:m + 1], in1=rows,
                                                           op0=ALU.add, op1=ALU.add).then_inc(final_done, 1)

                    dve.wait_ge(filled, B * FILLS + FIRST + I0)
                    statistics(0)
                    statistics(1)
                    if has_next:
                        scan_input(B + 1, 0, 0, 2)
                        scan_input(B + 1, 0, 1, 2)
                    for j in range(NCH):
                        for m in range(M):
                            dve.wait_ge(feat_ready, B * (2 * NCH) + 2 * j + m + 1)
                            nc.vector.tensor_tensor(feat[:, j % 2, m], feat[:, j % 2, m], xn[:, p, m, j * CH:(j + 1) * CH],
                                                    ALU.mult).then_inc(prod_ready, 1)
                        if j + 2 < NCH:
                            statistics(j + 2)
                        if j:
                            final(j - 1)
                        if has_next:
                            scan_up(0, j * (W // NCH), (j + 1) * (W // NCH))
                    final(NCH - 1)

                scan_input(NB * layer, 0, 0, 1)
                scan_up(0, 0, W)
                images(dve, layer, period, 1)

        @block.gpsimd
        def _(pool):
            pool.wait_ge(half_set, 1)
            for layer in range(LAYERS):
                pool.wait_ge(gn_var, layer + 1)
                for j in range(NCH):
                    rows = slice(j * HC, (j + 1) * HC)
                    nc.gpsimd.tensor_tensor(gscale[:, :, rows], per_row(gvar)[:, :, rows], per_row(mhalf[:])[:, :, rows],
                                            ALU.pow).then_inc(gn_pow, 1)

                def period(B, half_B, b, p, last):
                    for j in range(NCH):
                        s = j % 2
                        mean, var = mv[:, s, 3], mv[:, s, 5]
                        rstd, neg, shift = (ln[:, s, i] for i in range(3))
                        pool.wait_ge(mv_ready, B * NCH + j + 1)
                        nc.gpsimd.tensor_tensor(rstd, var, mhalf[:, 0:TT], ALU.pow).then_inc(ln_step, 1)
                        pool.wait_ge(ln_step, B * NCH + j + 1)
                        nc.gpsimd.tensor_tensor(neg, rstd, mone[:], ALU.mult)
                        nc.gpsimd.tensor_tensor(shift, mean, rstd, ALU.mult).then_inc(rstd_ready, 1)

                images(pool, layer, period, 0)


_WEIGHTS = ("Wg", "Wi", "Wl", "Wo")
_VECTORS = ("bg", "bi", "bl", "bo", "gamma", "beta")


def kernel(**inputs):
    import numpy as np
    import concourse.bacc as bacc
    from concourse.bass_utils import run_bass_kernel_spmd

    nc = bacc.Bacc("TRN2", target_bir_lowering=False, num_devices=1)
    arrays = {}

    def give(name, a):
        a = np.ascontiguousarray(a)
        arrays[name] = a
        return nc.dram_tensor(name, a.shape, mybir.dt.from_np(a.dtype), kind="ExternalInput").ap()

    x = give("x_cm", np.asarray(inputs["x"]).transpose(2, 3, 0, 1).reshape(NB, D, TOK))
    ws = [[give(f"w{layer}_{n}", np.asarray(inputs[f"L{layer}_conv_{n}"])) for layer in range(LAYERS)]
          for n in _WEIGHTS]
    vecs = [give(f"vecs{layer}", np.stack([np.asarray(inputs[f"L{layer}_conv_{n}"]).reshape(M, P)
                                           for n in _VECTORS]).transpose(2, 0, 1)) for layer in range(LAYERS)]
    ident = give("ident_c", np.eye(P, dtype=np.float32))
    gmat = give("gmat_c", np.kron(np.eye(P // GROUP), np.full((GROUP, GROUP), 1.0 / (GROUP * PARTS))).astype(np.float32))
    out = nc.dram_tensor("out_cm", (NB, D, TOK), F32, kind="ExternalOutput").ap()
    build(nc, x, *ws, vecs, ident, gmat, out)
    r = run_bass_kernel_spmd(nc, [arrays], core_ids=[0])
    y = np.asarray(r.results[0]["out_cm"])
    return np.ascontiguousarray(y.reshape(NB, D, H, W).transpose(2, 3, 0, 1))
```

```python
from contextlib import ExitStack

import concourse.bass as bass
from concourse import mybir

F32 = mybir.dt.float32
ALU = mybir.AluOpType
ACT = mybir.ActivationFunctionType
AX_X = mybir.AxisListType.X

P = 128
H, W, NB, D = 64, 64, 16, 256
M = D // P
TOK = H * W
CH = 512
NCH = TOK // CH
HC = CH // W
TT = CH // P
LAYERS = 2
GROUP = 8
GN_EPS, LN_EPS = 1e-5, 1e-5

SB = 8
NBG = NB // SB
STAT_UNITS = [[(bg, m) for bg in range(NBG) for m in range(M) if not (layer and (bg, m) == (0, 0))]
              for layer in range(LAYERS)]
STAT_BASE = [0, len(STAT_UNITS[0]) * NCH + 1]
PARTS = NBG * 2

FILLS = 2 * 3 * NCH
FIRST = 2 * NCH
ROWS = H * M
ROWS_CH = HC * M
SCAN_STEPS = 9
STORED = 16 * M
L1, I1, G, I0, L0 = 0, NCH, 2 * NCH, 4 * NCH, 5 * NCH
BG, BI, BL, BO, GAMMA, BETA = range(6)
EARLY = 2 * ROWS_CH
UP = 7
LATE = 4


def first_fills(inp, lam):
    return [(inp, j) for j in range(NCH // 2)] + [(lam, j) for j in range(NCH)] + \
           [(inp, j) for j in range(NCH // 2, NCH)]


def first_by_dve(h, m):
    return m == 0 or h % 2 == 0


def build(nc, x, w_g, w_i, w_l, w_o, vecs, ident_d, gmat_d, out):
    with ExitStack() as ctx:
        def sb(name, shape):
            return ctx.enter_context(nc.sbuf_tensor(name, shape, F32))

        def sem(name):
            return ctx.enter_context(nc.semaphore(name))

        xn = sb("xn", [P, 2, M, TOK])
        lam = sb("lam", [P, M, TOK])
        inp = sb("inp", [P, M, TOK])
        hid = sb("hid", [P, M, TOK])
        tmp = sb("tmp", [P, TOK])
        wg, wi, wl, wo = (sb(f"w{n}", [P, M, D]) for n in "gilo")
        vec = sb("vec", [P, 6, M])
        ident = sb("ident", [P, P])
        gmat = sb("gmat", [P, P])
        gscale = sb("gscale", [P, M, H])
        gshift = sb("gshift", [P, M, H])
        tail_mem = sb("tail_mem", [P, 2 * TT * D + 2 * M * CH])
        ntok = tail_mem[:, :2 * TT * D].rearrange("p (s t d) -> p s t d", s=2, t=TT)
        feat = tail_mem[:, 2 * TT * D:].rearrange("p (s m n) -> p s m n", s=2, m=M)
        early_mean = sb("early_mean", [P, H])
        early_m2 = sb("early_m2", [P, H])
        row_sum, row_mean = sb("row_sum", [P, HC]), sb("row_mean", [P, HC])
        lam0 = sb("lam0", [P, H])
        st = sb("st", [P, 2, TT, 6])
        mv = sb("mv", [P, 2, 5, TT])
        ln = sb("ln", [P, 2, 2, TT])
        consts = sb("consts", [P, 3, TT])
        c_minus_2, c_4_over_d, c_4_eps = (consts[:, i] for i in range(3))
        mhalf = sb("mhalf", [P, ROWS])

        res = [lam[:, 1], inp[:, 1]]
        NST = ROWS * NBG * 6
        parts = tmp[:, 0:NST].rearrange("p (m h g s) -> p m h g s", m=M, h=H, g=NBG)
        part = tmp[:, 0:NST].rearrange("p (r k s) -> p r k s", r=ROWS, k=PARTS)
        dev = tmp[:, NST:NST + ROWS * PARTS].rearrange("p (r k) -> p r k", r=ROWS)
        at = NST + ROWS * PARTS
        gsum, gmean, gdev, gm2, gq, gvar = (tmp[:, at + i * ROWS:at + (i + 1) * ROWS] for i in range(6))

        def per_row(t):
            return t.rearrange("p (m h) -> p m h", m=M)

        slots = xn[:].rearrange("p s m n -> p (s m) n")

        bank = [ctx.enter_context(nc.psum_tensor(f"bank{i}", [P, 512], F32)) for i in range(8)]
        fill_bank = bank[0:2]
        gate_bank = [bank[0:2], bank[6:8]]
        nchan_bank = bank[4:6]
        out_bank = bank[6:8]

        def htok_bank(j):
            return bank[2:4] if j % 2 == 0 else out_bank if j == 1 else fill_bank

        def proj_bank(j):
            return bank[2:4] if j == NCH - 2 else out_bank

        const_in, weights_in = sem("const_in"), sem("weights_in")
        stat_in = [sem(f"stat_in{i}") for i in range(M * NBG)]
        early_in, early_step, early_done = sem("early_in"), sem("early_step"), sem("early_done")
        stat_used, gn_sum, gn_mean, gn_link, gn_var, gn_pow, gn_ready = map(
            sem, ("stat_used", "gn_sum", "gn_mean", "gn_link", "gn_var", "gn_pow", "gn_ready"))
        x_in = [[sem(f"x_in{s}_{q}") for q in range(NCH // 2)] for s in range(2)]
        xn_ready, xn0_ready, fill_full, filled = map(sem, ("xn_ready", "xn0_ready", "fill_full", "filled"))
        res_in = [sem(f"res_in{i}") for i in range(NCH // 2)]
        out_stored = [sem(f"out_stored{i}") for i in range(NCH // 2)]
        scan_step, hid_begun, scans_done = sem("scan_step"), sem("hid_begun"), sem("scans_done")
        htok_full, stats_ready, ln_step, rstd_ready, ntok_ready = map(
            sem, ("htok_full", "stats_ready", "ln_step", "rstd_ready", "ntok_ready"))
        nchan_full, feat_ready, prod_ready, out_full, final_done = map(
            sem, ("nchan_full", "feat_ready", "prod_ready", "out_full", "final_done"))
        half_set = sem("half_set")

        mid = nc.dram_tensor("mid", [NB, D, TOK], F32, kind="Internal").ap()
        src, dst = [x, mid], [mid, out]

        block = ctx.enter_context(nc.Block())

        def images(eng, layer, period, last_pair_apart, take_up=False):
            def pair(g, last, **more):
                for p in range(2):
                    period(layer * NB + g * 2 + p, layer * (NB // 2) + g, g * 2 + p, p, last, **more)
            loops = NB // 2 - last_pair_apart
            if take_up:
                with eng.Fori(0, SB // 2) as g:
                    pair(g, False)
                with eng.Fori(SB // 2, loops) as g:
                    pair(g, False, takes_up=True)
                pair(loops, True, takes_up=True)
                return
            with eng.Fori(0, loops) as g:
                pair(g, False)
            if last_pair_apart:
                pair(loops, True)


        @block.sync
        def _(sp):
            sp.dma_start(ident[:], ident_d).then_inc(const_in, 16)
            sp.dma_start(gmat[:], gmat_d).then_inc(const_in, 16)

            for layer in range(LAYERS):
                xs, xd = src[layer], dst[layer]

                def image_rows(ap, b, a, n):
                    return ap[b].rearrange("(m p) t -> p m t", p=P)[:, :, a:a + n]

                def stat_rows(ap, hc, bg, m):
                    return ap.rearrange("(g b) (m p) (c n) -> g m p b c n", g=NBG, m=M, c=NCH)[bg, m][:, :, hc]

                def stat_unit(ap, hc, u, units):
                    sp.dma_start(slots[:, u].rearrange("p (b n) -> p b n", b=SB),
                                 stat_rows(ap, hc, *units[u])).then_inc(stat_in[u], 16)

                units = STAT_UNITS[layer]
                if layer:
                    for q in range(NCH // 2):
                        sp.wait_ge(out_stored[q], 16 + STORED * NB * layer)
                for u in range(1 if layer else 0, len(units)):
                    stat_unit(xs, 0, u, units)
                for t, d in ((wg, w_g), (wi, w_i), (wl, w_l), (wo, w_o)):
                    sp.dma_start(t[:], d[layer].rearrange("(k p) n -> p k n", p=P)).then_inc(weights_in, 16)
                sp.dma_start(vec[:], vecs[layer]).then_inc(weights_in, 16)
                with sp.Fori(1, NCH) as hc:
                    for u in range(len(units)):
                        sp.wait_ge(stat_used, hc * len(units) + STAT_BASE[layer] - len(units) + u + 1)
                        stat_unit(xs, hc, u, units)
                sp.wait_ge(stat_used, STAT_BASE[layer] + len(units) * NCH)

                def load_x(b, p, q):
                    sp.dma_start(xn[:, p, :, 2 * q * CH:2 * (q + 1) * CH],
                                 image_rows(xs, b, 2 * q * CH, 2 * CH)).then_inc(x_in[p][q], 16)

                def res_rows(ap, b, m, q):
                    return ap[b, m * P:(m + 1) * P, 2 * q * CH:2 * (q + 1) * CH]

                for b in range(2):
                    for q in range(NCH // 2):
                        load_x(b, b, q)

                def period(B, half_B, b, p, last, takes_up=False):
                    if takes_up:
                        for q in range(NCH // 2):
                            sp.wait_ge(out_stored[q], 16 + STORED * (NB * layer + SB))
                        sp.dma_start(tail_mem[:].rearrange("p (b n) -> p b n", b=SB),
                                     stat_rows(xd, b - SB, 0, 0)).then_inc(early_in, 16)
                    sp.wait_ge(scans_done, B * 2 + 3)
                    for q in range(NCH // 2):
                        for m in range(M):
                            sp.dma_start(res[m][:, 2 * q * CH:2 * (q + 1) * CH],
                                         res_rows(xs, b, m, q)).then_inc(res_in[q], 16)
                    if last and p and layer + 1 < LAYERS:
                        stat_unit(xd, 0, 0, STAT_UNITS[layer + 1])
                    for q in range(NCH // 2):
                        sp.wait_ge(final_done, B * (2 * NCH) + 4 * q + 4)
                        for m in range(M):
                            sp.dma_start(res_rows(xd, b, m, q),
                                         res[m][:, 2 * q * CH:2 * (q + 1) * CH]).then_inc(out_stored[q], 16)
                        if not last:
                            load_x(b + 2, p, q)

                images(sp, layer, period, 1, take_up=layer + 1 < LAYERS)

            for q in range(NCH // 2):
                sp.wait_ge(out_stored[q], 16 + STORED * NB * LAYERS)

        @block.tensor
        def _(pe):
            pe.wait_ge(const_in, 32)

            def project_in(w, m, p, j, to):
                for k in range(M):
                    last = nc.tensor.matmul(to[:], w[:, k, m * P:(m + 1) * P],
                                            xn[:, p, k, j * CH:(j + 1) * CH], start=(k == 0), stop=(k == M - 1))
                last.then_inc(fill_full, 1)

            def fill(w, m, p, group, normed=None, first=0, end=NCH, after_gates=False):
                for j in range(first, end):
                    if normed is not None:
                        pe.wait_ge(xn_ready, normed + j + 1)
                    pe.wait_ge(filled, group + j - (3 if after_gates and j < 2 else 1))
                    project_in(w, m, p, j, fill_bank[j % 2])

            def fill_gates(p, group):
                for j in range(NCH):
                    for m in range(M):
                        if j == 0:
                            pe.wait_ge(filled, group - 1 + m)
                        elif j > 1:
                            pe.wait_ge(filled, group + 2 * (j - 2) + m + 1)
                        project_in(wg, m, p, j, gate_bank[j % 2][m])

            for layer in range(LAYERS):
                pe.wait_ge(gn_sum, 2 * layer + 1)
                nc.tensor.matmul(bank[2][:, 0:ROWS], gmat[:], gsum, start=True, stop=True).then_inc(gn_mean, 1)
                pe.wait_ge(gn_sum, 2 * layer + 2)
                nc.tensor.matmul(bank[3][:, 0:ROWS], gmat[:], gq, start=True, stop=True).then_inc(gn_mean, 1)

                pe.wait_ge(weights_in, 80 * (layer + 1))
                group = FILLS * NB * layer
                for g, (w, j) in enumerate(first_fills(wi, wl)):
                    pe.wait_ge(xn0_ready, NCH * layer + j + 1)
                    pe.wait_ge(xn_ready, NCH * NB * layer + j + 1)
                    if group + g > 1:
                        pe.wait_ge(filled, group + g - 1)
                    project_in(w, 0, 0, j, fill_bank[g % 2])

                def to_tokens(B, j):
                    for t in range(TT):
                        a = j * CH + t * P
                        for m in range(M):
                            last = nc.tensor.transpose(
                                htok_bank(j)[t // 2][:, (t % 2) * D + m * P:(t % 2) * D + (m + 1) * P],
                                hid[:, m, a:a + P], ident[:])
                    last.then_inc(htok_full, 1)

                def project(B, j):
                    pe.wait_ge(prod_ready, B * (2 * NCH) + 2 * j + 2)
                    for m in range(M):
                        if j and proj_bank(j) is out_bank:
                            before = j - 2 if j == NCH - 1 else j - 1
                            pe.wait_ge(final_done, B * (2 * NCH) + 2 * before + m + 1)
                        for k in range(M):
                            last = nc.tensor.matmul(proj_bank(j)[m][:], wo[:, k, m * P:(m + 1) * P],
                                                    feat[:, j % 2, k], start=(k == 0), stop=(k == M - 1))
                        last.then_inc(out_full, 1)

                def period(B, half_B, b, p, last):
                    group = B * FILLS + FIRST
                    has_next = not (last and p)
                    fill(wl, 1, p, group + L1)
                    fill(wi, 1, p, group + I1)
                    fill_gates(p, group + G)
                    if has_next:
                        fill(wi, 0, 1 - p, group + I0, B * NCH + NCH, after_gates=True)
                        fill(wl, 0, 1 - p, group + L0, end=NCH - LATE)
                    pe.wait_ge(hid_begun, B * 2 + 2)
                    pe.wait_ge(filled, group + I0)
                    to_tokens(B, 0)
                    to_tokens(B, 1)
                    if has_next:
                        fill(wl, 0, 1 - p, group + L0, first=NCH - LATE, end=NCH - 1)
                    for j in range(NCH):
                        pe.wait_ge(ntok_ready, B * NCH + j + 1)
                        for m in range(M):
                            if j:
                                pe.wait_ge(feat_ready, B * (2 * NCH) + 2 * j - 2 + m + 1)
                            for t in range(TT):
                                last_t = nc.tensor.transpose(nchan_bank[m][:, t * P:(t + 1) * P],
                                                             ntok[:, j % 2, t, m * P:(m + 1) * P], ident[:])
                            last_t.then_inc(nchan_full, 1)
                        if j + 2 < NCH:
                            if j == 0:
                                pe.wait_ge(scans_done, B * 2 + 3)
                            if j == 1:
                                pe.wait_ge(filled, group + (FILLS if has_next else FILLS - FIRST))
                            to_tokens(B, j + 2)
                        if j == 0 and has_next:
                            fill(wl, 0, 1 - p, group + L0, first=NCH - 1)
                        if j:
                            project(B, j - 1)
                    project(B, NCH - 1)

                images(pe, layer, period, 1)

        @block.scalar
        def _(act):
            for layer in range(LAYERS):
                act.wait_ge(weights_in, 80 * (layer + 1))

                def normalise(half_B, p, first, count, is_first=False):
                    for r in range(first, first + count):
                        h, m = r // M, r % M
                        if r % (2 * ROWS_CH) == 0:
                            act.wait_ge(x_in[p][r // (2 * ROWS_CH)], half_B * 16 + 16)
                        if is_first:
                            if r % ROWS_CH == 0:
                                act.wait_ge(gn_ready, NCH * layer + h // HC + 1)
                            if first_by_dve(h, m):
                                continue
                        row = xn[:, p, m, h * W:(h + 1) * W]
                        ins = nc.scalar.activation(row, row, ACT.Identity, bias=gshift[:, m, h:h + 1],
                                                   scale=gscale[:, m, h:h + 1])
                        if r % ROWS_CH == ROWS_CH - 1:
                            ins.then_inc(xn_ready, 1)

                def evacuate(j, group, func, bias, m, to):
                    act.wait_ge(fill_full, group + j + 1)
                    nc.scalar.activation(to, fill_bank[j % 2][:], func, bias=vec[:, bias, m:m + 1]).then_inc(filled, 1)

                def chunk(t, m, j):
                    return t[:, m, j * CH:(j + 1) * CH]

                B0 = NB * layer
                normalise(B0 // 2, 0, 0, 2 * ROWS_CH, True)
                for g, (t, j) in enumerate(first_fills(inp, lam)):
                    act.wait_ge(fill_full, FILLS * B0 + g + 1)
                    nc.scalar.activation(chunk(t, 0, j), fill_bank[g % 2][:], ACT.Sigmoid if t is lam else ACT.Silu,
                                         bias=vec[:, BL if t is lam else BI, 0:1]).then_inc(filled, 1)
                    if g + 2 < NCH:
                        normalise(B0 // 2, 0, ROWS_CH * (g + 2), ROWS_CH, True)
                    else:
                        normalise(B0 // 2, 1, 3 * (g + 2 - NCH), 3)
                done = 3 * (len(first_fills(inp, lam)) + 2 - NCH)
                normalise(B0 // 2, 1, done, EARLY - done)

                def take_up(b, step):
                    def per_h(t, h, n):
                        return t[:, bass.ds((b - SB) * HC + h, n)]

                    rows = tail_mem[:].rearrange("p (b h w) -> p h b w", b=SB, w=W)
                    if step == 0:
                        act.wait_ge(early_in, b * 16 - 16 * (SB - 1))
                    if step < HC:
                        nc.scalar.activation(rows[:, step], rows[:, step], ACT.Identity,
                                             accum_out=row_sum[:, step:step + 1]).then_inc(early_step, 1)
                    elif step == HC:
                        act.wait_ge(early_step, b * (HC + 1) - (HC + 1) * SB + HC)
                        nc.scalar.activation(row_mean[:], row_sum[:], ACT.Identity,
                                             scale=-1.0 / (SB * W)).then_inc(early_step, 1)
                    elif step == HC + 1:
                        nc.scalar.activation(per_h(early_mean, 0, HC), row_mean[:], ACT.Identity).then_inc(early_done, 1)
                    else:
                        h = step - HC - 2
                        nc.scalar.activation(rows[:, h], rows[:, h], ACT.Square, bias=row_mean[:, h:h + 1],
                                             accum_out=per_h(early_m2, h, 1)).then_inc(early_done, 1)

                def period(B, half_B, b, p, last, takes_up=False):
                    group = B * FILLS + FIRST
                    has_next = not (last and p)
                    steps = iter(range(2 * HC + 2) if takes_up else ())

                    def take_up_some(n):
                        for step in steps:
                            take_up(b, step)
                            n -= 1
                            if step == HC:
                                act.wait_ge(early_step, b * (HC + 1) - (HC + 1) * SB + HC + 1)
                            if step == HC or n == 0:
                                return

                    rows_done = [EARLY]

                    def normalise_next(count):
                        if has_next:
                            normalise(half_B + p, 1 - p, rows_done[0], count)
                            rows_done[0] += count

                    for j in range(NCH):
                        if j % 2 == 0:
                            act.wait_ge(out_stored[j // 2], B * STORED + 16)
                        evacuate(j, group + L1, ACT.Sigmoid, BL, 1, chunk(lam, 1, j))
                        normalise_next(3)
                    for j in range(NCH):
                        evacuate(j, group + I1, ACT.Silu, BI, 1, chunk(inp, 1, j))
                        normalise_next(3)
                    for j in range(NCH):
                        act.wait_ge(fill_full, group + G + 2 * j + 2)
                        for m in range(M):
                            nc.scalar.activation(xn[:, p, m, j * CH:(j + 1) * CH], gate_bank[j % 2][m][:], ACT.Silu,
                                                 bias=vec[:, BG, m:m + 1]).then_inc(filled, 1)
                        normalise_next(6 if j < NCH - 1 else 2)
                    if has_next:
                        act.wait_ge(scans_done, B * 2 + 2)
                        for j in range(NCH):
                            evacuate(j, group + I0, ACT.Silu, BI, 0, chunk(inp, 0, j))
                            if rows_done[0] < ROWS:
                                normalise_next(2)
                            take_up_some(1 if j < 2 else 2)
                        for j in range(NCH - LATE + 1):
                            evacuate(j, group + L0, ACT.Sigmoid, BL, 0, chunk(lam, 0, j))
                            take_up_some(1 if j else 2)
                    take_up_some(2 * HC)
                    take_up_some(2 * HC)
                    if takes_up:
                        act.wait_ge(early_done, b * (HC + 1) - (HC + 1) * (SB - 1))

                    def layer_norm(j):
                        act.wait_ge(rstd_ready, B * NCH + j + 1)
                        for t in range(TT):
                            ins = nc.scalar.activation(
                                ntok[:, j % 2, t], htok_bank(j)[t // 2][:, (t % 2) * D:(t % 2 + 1) * D], ACT.Identity,
                                bias=ln[:, j % 2, 1, t:t + 1], scale=ln[:, j % 2, 0, t:t + 1])
                        ins.then_inc(ntok_ready, 1)

                    layer_norm(0)
                    if has_next:
                        for j in range(NCH - LATE + 1, NCH - 1):
                            evacuate(j, group + L0, ACT.Sigmoid, BL, 0, chunk(lam, 0, j))
                    layer_norm(1)
                    for j in range(NCH):
                        for m in range(M):
                            act.wait_ge(nchan_full, B * (2 * NCH) + 2 * j + m + 1)
                            nc.scalar.activation(feat[:, j % 2, m], nchan_bank[m][:], ACT.Identity,
                                                 bias=vec[:, BETA, m:m + 1],
                                                 scale=vec[:, GAMMA, m:m + 1]).then_inc(feat_ready, 1)
                        if 1 < j + 1 < NCH:
                            layer_norm(j + 1)
                        if j == 0 and has_next:
                            evacuate(NCH - 1, group + L0, ACT.Sigmoid, BL, 0, chunk(lam, 0, NCH - 1))
                        if not last and j == NCH - 3:
                            normalise(half_B + 1, p, 0, ROWS_CH // 2)
                        if not last and j == NCH - 2:
                            normalise(half_B + 1, p, ROWS_CH // 2, 3)
                    if not last:
                        normalise(half_B + 1, p, ROWS_CH // 2 + 3, EARLY - ROWS_CH // 2 - 3)

                images(act, layer, period, 1, take_up=layer + 1 < LAYERS)

        @block.vector
        def _(dve):
            nc.vector.memset(c_minus_2, -2.0)
            nc.vector.memset(c_4_over_d, 4.0 / D)
            nc.vector.memset(c_4_eps, 4.0 * LN_EPS)
            nc.vector.memset(mhalf[:], -0.5).then_inc(half_set, 1)
            nc.vector.memset(lam0[:], 0.0).then_inc(scans_done, 1)
            for q in range(NCH // 2):
                nc.vector.memset(st[:, 0, q], 0.0).then_inc(out_stored[q], 16)
            gn_at = [0]

            for layer in range(LAYERS):
                if layer:
                    dve.wait_ge(early_done, NCH * (HC + 1) * layer)
                    for k in (0, 3):
                        nc.vector.tensor_scalar(parts[:, 0, :, 0, k + 1], early_mean[:], -1.0, None, ALU.mult)
                        ins = nc.vector.tensor_scalar(parts[:, 0, :, 0, k + 2], early_m2[:], 0.5, None, ALU.mult)
                    ins.then_inc(stat_used, 1)
                with dve.Fori(0, NCH) as hc:
                    for u, (bg, m) in enumerate(STAT_UNITS[layer]):
                        dve.wait_ge(stat_in[u], hc * 16 + 16 * (NCH * layer + 1))
                        rows = slots[:, u].rearrange("p (b h w) -> p h b w", b=SB, w=W)
                        for h in range(HC):
                            ins = nc.vector.bn_stats(parts[:, m, bass.ds(hc * HC + h, 1), bg].rearrange("p a s -> p (a s)"),
                                                     rows[:, h])
                        ins.then_inc(stat_used, 1)
                dve.wait_ge(stat_used, STAT_BASE[layer] + len(STAT_UNITS[layer]) * NCH)

                def link(ins):
                    ins.then_inc(gn_link, 1)
                    gn_at[0] += 1
                    dve.wait_ge(gn_link, gn_at[0])

                mean_k, m2_k = part[:, :, :, 1], part[:, :, :, 2]
                nc.vector.tensor_reduce(gsum, mean_k, AX_X, ALU.add).then_inc(gn_sum, 1)
                dve.wait_ge(gn_mean, 2 * layer + 1)
                link(nc.vector.tensor_copy(gmean, bank[2][:, 0:ROWS]))
                link(nc.vector.tensor_tensor(dev, mean_k, gmean.unsqueeze(2).broadcast_to((P, ROWS, PARTS)),
                                             ALU.subtract))
                link(nc.vector.tensor_tensor(dev, dev, dev, ALU.mult))
                link(nc.vector.tensor_reduce(gdev, dev, AX_X, ALU.add))
                link(nc.vector.tensor_reduce(gm2, m2_k, AX_X, ALU.add))
                nc.vector.scalar_tensor_tensor(out=gq, in0=gm2, scalar=1.0 / (SB * W // 2), in1=gdev, op0=ALU.mult,
                                               op1=ALU.add).then_inc(gn_sum, 1)
                dve.wait_ge(gn_mean, 2 * layer + 2)
                nc.vector.tensor_scalar(gvar, bank[3][:, 0:ROWS], GN_EPS, None, ALU.add).then_inc(gn_var, 1)
                for j in range(NCH):
                    dve.wait_ge(gn_pow, NCH * layer + j + 1)
                    rows = slice(j * HC, (j + 1) * HC)
                    nc.vector.scalar_tensor_tensor(out=gshift[:, :, rows], in0=per_row(gmean)[:, :, rows], scalar=-1.0,
                                                   in1=gscale[:, :, rows], op0=ALU.mult,
                                                   op1=ALU.mult).then_inc(gn_ready, 1)
                    dve.wait_ge(gn_ready, NCH * layer + j + 1)
                    if j % 2 == 0:
                        dve.wait_ge(x_in[0][j // 2], 16 * (NB // 2 * layer + 1))
                    for h in range(j * HC, (j + 1) * HC):
                        for m in range(M):
                            if first_by_dve(h, m):
                                row = xn[:, 0, m, h * W:(h + 1) * W]
                                ins = nc.vector.tensor_scalar(row, row, gscale[:, m, h:h + 1], gshift[:, m, h:h + 1],
                                                              ALU.mult, ALU.add)
                    ins.then_inc(xn0_ready, 1)

                def columns(t):
                    return t.rearrange("p (h w) -> p w h", w=W)

                def scan_input(B, m, part, parts):
                    dve.wait_ge(filled, B * FILLS + (FIRST if m == 0 else FIRST + G) - (parts - 1 - part) * NCH // parts)
                    tokens = slice(part * TOK // parts, (part + 1) * TOK // parts)
                    ins = nc.vector.scalar_tensor_tensor(out=inp[:, m, tokens], in0=lam[:, m, tokens], scalar=1.0,
                                                         in1=inp[:, m, tokens], op0=ALU.subtract, op1=ALU.mult)
                    if part == parts - 1:
                        ins.then_inc(scan_step, 1)
                        dve.wait_ge(scan_step, (B * 2 + m) * SCAN_STEPS + 1)

                def scan_up(m, some):
                    Lc, Ic, Tc = (columns(t) for t in (lam[:, m], inp[:, m], tmp[:]))
                    for w in some:
                        nc.vector.tensor_tensor_scan(Tc[:, w, ::-1], Lc[:, w, ::-1], Ic[:, w, ::-1], 0.0,
                                                     ALU.mult, ALU.add)

                def scans(B, m):
                    L, I, S = lam[:, m], inp[:, m], hid[:, m]
                    base = (B * 2 + m) * SCAN_STEPS
                    Lc, Ic, Sc = (columns(t) for t in (L, I, S))
                    for w in range(W):
                        nc.vector.tensor_tensor_scan(Sc[:, w], Lc[:, w], Ic[:, w], 0.0, ALU.mult, ALU.add)
                    nc.vector.tensor_copy(lam0[:], Lc[:, 0]).then_inc(scan_step, 1)
                    dve.wait_ge(scan_step, base + 2)
                    nc.vector.memset(Lc[:, 0], 0.0).then_inc(scan_step, 1)
                    nc.vector.tensor_tensor(S, S, tmp[:], ALU.add).then_inc(scan_step, 1)
                    dve.wait_ge(scan_step, base + 4)
                    nc.vector.tensor_tensor_scan(tmp[:], L, I, 0.0, ALU.mult, ALU.add).then_inc(scan_step, 1)
                    dve.wait_ge(scan_step, base + 5)
                    nc.vector.tensor_copy(Lc[:, 0], lam0[:]).then_inc(scan_step, 1)
                    nc.vector.memset(Lc[:, W - 1], 0.0).then_inc(scan_step, 1)
                    nc.vector.tensor_tensor(S, S, tmp[:], ALU.add).then_inc(scan_step, 1)
                    dve.wait_ge(scan_step, base + 8)
                    nc.vector.tensor_tensor_scan(tmp[:, ::-1], L[:, ::-1], I[:, ::-1], 0.0, ALU.mult,
                                                 ALU.add).then_inc(scan_step, 1)
                    dve.wait_ge(scan_step, base + 9)
                    nc.vector.tensor_tensor(S[:, :2 * CH], S[:, :2 * CH], tmp[:, :2 * CH],
                                            ALU.add).then_inc(hid_begun, 1)
                    nc.vector.tensor_tensor(S[:, 2 * CH:], S[:, 2 * CH:], tmp[:, 2 * CH:],
                                            ALU.add).then_inc(scans_done, 1)

                def period(B, half_B, b, p, last):
                    has_next = not (last and p)
                    scans(B, 0)
                    scan_input(B, 1, 0, 1)
                    dve.wait_ge(scans_done, B * 2 + 2)
                    scan_up(1, range(W))
                    scans(B, 1)

                    def statistics(j):
                        dve.wait_ge(htok_full, B * NCH + j + 1)
                        for t in range(TT):
                            ins = nc.vector.bn_stats(st[:, j % 2, t],
                                                     htok_bank(j)[t // 2][:, (t % 2) * D:(t % 2 + 1) * D])
                        ins.then_inc(stats_ready, 1)

                    def final(j, m):
                        dve.wait_ge(res_in[j // 2], B * 32 + 32)
                        dve.wait_ge(out_full, B * (2 * NCH) + 2 * j + m + 1)
                        rows = res[m][:, j * CH:(j + 1) * CH]
                        nc.vector.scalar_tensor_tensor(out=rows, in0=proj_bank(j)[m][:], scalar=vec[:, BO, m:m + 1],
                                                       in1=rows, op0=ALU.add, op1=ALU.add).then_inc(final_done, 1)

                    dve.wait_ge(filled, B * FILLS + FIRST + I0)
                    for j in range(2):
                        statistics(j)
                    if has_next:
                        for quarter in range(3):
                            scan_input(B + 1, 0, quarter, 4)
                    for j in range(NCH):
                        if j + 2 < NCH:
                            statistics(j + 2)
                        for m in range(M):
                            dve.wait_ge(feat_ready, B * (2 * NCH) + 2 * j + m + 1)
                            nc.vector.tensor_tensor(feat[:, j % 2, m], feat[:, j % 2, m], xn[:, p, m, j * CH:(j + 1) * CH],
                                                    ALU.mult).then_inc(prod_ready, 1)
                        if j == 0 and has_next:
                            scan_input(B + 1, 0, 3, 4)
                        columns_now = range(j * UP, (j + 1) * UP if j + 1 < NCH else W)
                        first_columns = UP if j >= NCH - 2 else 0
                        if has_next:
                            scan_up(0, columns_now[:first_columns])
                        if j:
                            final(j - 1, 0)
                        if has_next:
                            scan_up(0, columns_now[first_columns:UP])
                        if j:
                            final(j - 1, 1)
                        if has_next:
                            scan_up(0, columns_now[UP:])
                    for m in range(M):
                        final(NCH - 1, m)

                for quarter in range(4):
                    scan_input(NB * layer, 0, quarter, 4)
                scan_up(0, range(W))
                images(dve, layer, period, 1)

        @block.gpsimd
        def _(pool):
            pool.wait_ge(half_set, 1)
            for layer in range(LAYERS):
                pool.wait_ge(gn_var, layer + 1)
                for j in range(NCH):
                    rows = slice(j * HC, (j + 1) * HC)
                    nc.gpsimd.tensor_tensor(gscale[:, :, rows], per_row(gvar)[:, :, rows], per_row(mhalf[:])[:, :, rows],
                                            ALU.pow).then_inc(gn_pow, 1)

                def period(B, half_B, b, p, last):
                    for j in range(NCH):
                        s = j % 2
                        _, mean_e, m2_e, _, mean_o, m2_o = (st[:, s, :, i] for i in range(6))
                        total, diff, m2, var4, half = (mv[:, s, i] for i in range(5))
                        neg, shift = ln[:, s, 0], ln[:, s, 1]
                        at = B * (5 * NCH) + 5 * j
                        pool.wait_ge(stats_ready, B * NCH + j + 1)
                        nc.gpsimd.tensor_tensor(diff, mean_e, mean_o, ALU.subtract)
                        nc.gpsimd.tensor_tensor(m2, m2_e, m2_o, ALU.add).then_inc(ln_step, 1)
                        nc.gpsimd.tensor_tensor(total, mean_e, mean_o, ALU.add)
                        pool.wait_ge(ln_step, at + 1)
                        nc.gpsimd.tensor_tensor(diff, diff, diff, ALU.mult)
                        nc.gpsimd.tensor_tensor(m2, m2, c_4_over_d, ALU.mult).then_inc(ln_step, 1)
                        pool.wait_ge(ln_step, at + 2)
                        nc.gpsimd.tensor_tensor(var4, m2, diff, ALU.add).then_inc(ln_step, 1)
                        pool.wait_ge(ln_step, at + 3)
                        nc.gpsimd.tensor_tensor(var4, var4, c_4_eps, ALU.add).then_inc(ln_step, 1)
                        pool.wait_ge(ln_step, at + 4)
                        nc.gpsimd.tensor_tensor(half, var4, mhalf[:, 0:TT], ALU.pow).then_inc(ln_step, 1)
                        pool.wait_ge(ln_step, at + 5)
                        nc.gpsimd.tensor_tensor(neg, half, c_minus_2, ALU.mult)
                        nc.gpsimd.tensor_tensor(shift, total, half, ALU.mult).then_inc(rstd_ready, 1)

                images(pool, layer, period, 0)


_WEIGHTS = ("Wg", "Wi", "Wl", "Wo")
_VECTORS = ("bg", "bi", "bl", "bo", "gamma", "beta")


def kernel(**inputs):
    import numpy as np
    import concourse.bacc as bacc
    from concourse.bass_utils import run_bass_kernel_spmd

    nc = bacc.Bacc("TRN2", target_bir_lowering=False, num_devices=1)
    arrays = {}

    def give(name, a):
        a = np.ascontiguousarray(a)
        arrays[name] = a
        return nc.dram_tensor(name, a.shape, mybir.dt.from_np(a.dtype), kind="ExternalInput").ap()

    x = give("x_cm", np.asarray(inputs["x"]).transpose(2, 3, 0, 1).reshape(NB, D, TOK))
    ws = [[give(f"w{layer}_{n}", np.asarray(inputs[f"L{layer}_conv_{n}"])) for layer in range(LAYERS)]
          for n in _WEIGHTS]
    vecs = [give(f"vecs{layer}", np.stack([np.asarray(inputs[f"L{layer}_conv_{n}"]).reshape(M, P)
                                           for n in _VECTORS]).transpose(2, 0, 1)) for layer in range(LAYERS)]
    ident = give("ident_c", np.eye(P, dtype=np.float32))
    gmat = give("gmat_c", np.kron(np.eye(P // GROUP), np.full((GROUP, GROUP), 1.0 / (GROUP * PARTS))).astype(np.float32))
    out = nc.dram_tensor("out_cm", (NB, D, TOK), F32, kind="ExternalOutput").ap()
    build(nc, x, *ws, vecs, ident, gmat, out)
    r = run_bass_kernel_spmd(nc, [arrays], core_ids=[0])
    y = np.asarray(r.results[0]["out_cm"])
    return np.ascontiguousarray(y.reshape(NB, D, H, W).transpose(2, 3, 0, 1))
```
